# Optimizing a Trainium2 kernel written in Bass

```python
import numpy as np
import jax
import jax.numpy as jnp

def _softmax(x, axis=-1):
    return jax.nn.softmax(x, axis=axis)

def _gelu(x):
    return jax.nn.gelu(x, approximate=True)

def _silu(x):
    return jax.nn.silu(x)

def _sigmoid(x):
    return jax.nn.sigmoid(x)

def _layernorm(x, axis=-1, eps=1e-05):
    m = jnp.mean(x, axis=axis, keepdims=True)
    v = jnp.var(x, axis=axis, keepdims=True)
    return (x - m) / jnp.sqrt(v + eps)

def _scatter_add(tgt, idx, src, axis=0):
    return tgt.at[idx].add(src)

def _segment_sum(src, seg, n):
    return jax.ops.segment_sum(src, seg, n)
kernel_name = 'mk_gnn_resnorm_d1_gnn_r8_75daa1'

def setup_inputs(seed: int=0):
    np.random.seed(seed)
    _w = jnp.asarray

    def _rec_inputs():
        import jax
        import jax.numpy as jnp
        _gk = jax.random.key(seed)
        x = -6.415e-05 + 1 * jax.random.normal(jax.random.fold_in(_gk, 1), (6250, 512), jnp.float32)
        src = jax.random.randint(jax.random.fold_in(_gk, 2), (100000,), 0, 6250, jnp.int32)
        dst = jax.random.randint(jax.random.fold_in(_gk, 3), (100000,), 0, 6250, jnp.int32)
        _o = jnp.argsort(dst, stable=True)
        src = src[_o]
        dst = dst[_o]
        return (x, src, dst)
    x, src, dst = _rec_inputs()

    def _L0_gnn_setup():
        import jax, jax.numpy as jnp
        import numpy as np
        N, E, DM, H, DFF = (2500, 80000, 512, 8, 256)
        DK = DM // H

        def _layernorm(x, g, b, eps=1e-05):
            mu = jnp.mean(x, axis=-1, keepdims=True)
            var = jnp.mean(jnp.square(x - mu), axis=-1, keepdims=True)
            return (x - mu) * jax.lax.rsqrt(var + eps) * g + b
        key = jax.random.key(seed)
        ks = jax.random.split(key, 12)
        s = 0.02
        h = jax.random.normal(ks[0], (N, DM), dtype=jnp.float32)
        src = jax.random.randint(ks[1], (E,), 0, N, dtype=jnp.int32)
        dst = jnp.sort(jax.random.randint(ks[2], (E,), 0, N, dtype=jnp.int32))
        return {'h': h, 'src': src, 'dst': dst, 'Wq': jax.random.normal(ks[3], (DM, DM), dtype=jnp.float32) * s, 'Wk': jax.random.normal(ks[4], (DM, DM), dtype=jnp.float32) * s, 'Wv': jax.random.normal(ks[5], (DM, DM), dtype=jnp.float32) * s, 'Wo': jax.random.normal(ks[6], (DM, DM), dtype=jnp.float32) * s, 'ln1_g': jnp.ones((DM,), jnp.float32), 'ln1_b': jnp.zeros((DM,), jnp.float32), 'ln2_g': jnp.ones((DM,), jnp.float32), 'ln2_b': jnp.zeros((DM,), jnp.float32), 'W1': jax.random.normal(ks[7], (DM, DFF), dtype=jnp.float32) * s, 'b1': jnp.zeros((DFF,), jnp.float32), 'W2': jax.random.normal(ks[8], (DFF, DM), dtype=jnp.float32) * s, 'b2': jnp.zeros((DM,), jnp.float32)}
    _L0_gnn_all = _L0_gnn_setup()
    _L0_gnn_in = {k: v for k, v in _L0_gnn_all.items() if k in ('Wq', 'Wk', 'Wv', 'Wo', 'ln1_g', 'ln1_b', 'ln2_g', 'ln2_b', 'W1', 'b1', 'W2', 'b2')}
    del _L0_gnn_all
    return {'x': x, 'src': src, 'dst': dst, 'L0_gnn_Wq': _L0_gnn_in['Wq'], 'L0_gnn_Wk': _L0_gnn_in['Wk'], 'L0_gnn_Wv': _L0_gnn_in['Wv'], 'L0_gnn_Wo': _L0_gnn_in['Wo'], 'L0_gnn_ln1_g': _L0_gnn_in['ln1_g'], 'L0_gnn_ln1_b': _L0_gnn_in['ln1_b'], 'L0_gnn_ln2_g': _L0_gnn_in['ln2_g'], 'L0_gnn_ln2_b': _L0_gnn_in['ln2_b'], 'L0_gnn_W1': _L0_gnn_in['W1'], 'L0_gnn_b1': _L0_gnn_in['b1'], 'L0_gnn_W2': _L0_gnn_in['W2'], 'L0_gnn_b2': _L0_gnn_in['b2']}

def reference(x, src, dst, L0_gnn_Wq, L0_gnn_Wk, L0_gnn_Wv, L0_gnn_Wo, L0_gnn_ln1_g, L0_gnn_ln1_b, L0_gnn_ln2_g, L0_gnn_ln2_b, L0_gnn_W1, L0_gnn_b1, L0_gnn_W2, L0_gnn_b2):
    import jax
    import jax.numpy as jnp

    def _L0_gnn_ref(h, src, dst, Wq, Wk, Wv, Wo, ln1_g, ln1_b, ln2_g, ln2_b, W1, b1, W2, b2):
        import jax, jax.numpy as jnp
        import numpy as np
        N, E, DM, H, DFF = (2500, 80000, 512, 8, 256)
        DK = DM // H

        def _layernorm(x, g, b, eps=1e-05):
            mu = jnp.mean(x, axis=-1, keepdims=True)
            var = jnp.mean(jnp.square(x - mu), axis=-1, keepdims=True)
            return (x - mu) * jax.lax.rsqrt(var + eps) * g + b
        n = h.shape[0]
        q = (h @ Wq).reshape(n, H, DK)
        k = (h @ Wk).reshape(n, H, DK)
        v = (h @ Wv).reshape(n, H, DK)
        e = jnp.einsum('ehd,ehd->eh', k[src], q[dst]) / np.sqrt(DK).astype(np.float32)
        m = jax.ops.segment_max(e, dst, num_segments=n)
        ex = jnp.exp(e - m[dst])
        z = jax.ops.segment_sum(ex, dst, num_segments=n)
        attn = ex / z[dst]
        a = jax.ops.segment_sum(attn[:, :, None] * v[src], dst, num_segments=n)
        a = a.reshape(n, DM)
        o = a @ Wo
        x = _layernorm(h + o, ln1_g, ln1_b)
        f = jax.nn.relu(x @ W1 + b1) @ W2 + b2
        return _layernorm(x + f, ln2_g, ln2_b)
    x = _layernorm(x + _L0_gnn_ref(x, src, dst, L0_gnn_Wq, L0_gnn_Wk, L0_gnn_Wv, L0_gnn_Wo, L0_gnn_ln1_g, L0_gnn_ln1_b, L0_gnn_ln2_g, L0_gnn_ln2_b, L0_gnn_W1, L0_gnn_b1, L0_gnn_W2, L0_gnn_b2), axis=-1)
    return x

_drawn_inputs = setup_inputs


def setup_inputs(seed=0):
    import zlib

    import numpy as np

    out = dict(_drawn_inputs(seed))
    spreads = {'L0_gnn_ln1_g': (1.0, 0.2),
     'L0_gnn_ln1_b': (0.0, 0.1),
     'L0_gnn_ln2_g': (1.0, 0.2),
     'L0_gnn_ln2_b': (0.0, 0.1),
     'L0_gnn_b1': (0.0, 0.752),
     'L0_gnn_b2': (0.0, 0.1)}
    factors = {'L0_gnn_Wq': 8.0, 'L0_gnn_Wk': 8.0}
    for name, (base, spread) in spreads.items():
        noise = np.random.default_rng([zlib.crc32(name.encode()), seed]).standard_normal(out[name].shape)
        drawn = base * np.exp(spread * noise) if base else spread * noise
        out[name] = jnp.asarray(drawn.astype(out[name].dtype))
    for name, factor in factors.items():
        out[name] = (out[name] * factor).astype(out[name].dtype)
    return out
```

```python
import concourse.bass as bass
from concourse import mybir
from contextlib import ExitStack

P = 128
NODES, EDGES, D, HEADS, DFF = 6250, 100000, 512, 8, 256
DK = D // HEADS
KC = D // P
FC = DFF // P
BLOCKS = -(-NODES // P)
TILES = 784
STEPS = 832
UN = 16
RUNS = 16
RL = STEPS // RUNS
RE = RL * P
GROUPS = 7
TROWS = GROUPS * P
XT = 53
W = D + HEADS
RING = 8
SKIP = 20000
BIG = 2.0 ** 126
EPS = 1e-5
DVH = 5


def program(nc, a, out):
    f32, bf16, i32 = mybir.dt.float32, mybir.dt.bfloat16, mybir.dt.int32
    ALU, ACT, AX = mybir.AluOpType, mybir.ActivationFunctionType, mybir.AxisListType
    ds = bass.ds
    ctx = ExitStack()

    def sb(name, shape, dt=f32):
        return ctx.enter_context(nc.sbuf_tensor(name, shape, dt))

    def sem(name):
        return ctx.enter_context(nc.semaphore(name))

    def wait(eng, s, n):
        if not isinstance(n, int) or n > 0:
            eng.wait_ge(s, n)
            if eng is nc.gpsimd and not isinstance(n, int):
                eng.nop(nofuse=True)

    def repeat(eng, n, body, start=0):
        body(start)
        with eng.Fori(start + 1, n) as i:
            body(i)

    def load8(eng, regs, table, at):
        eng.load(regs, table[0:1, ds(at, 8)])
        return [eng.snap(r, min_val=0, max_val=BLOCKS - 1) for r in regs]

    def wait(eng, s, n):
        if not isinstance(n, int) or n > 0:
            eng.wait_ge(s, n)
            if eng is nc.gpsimd and not isinstance(n, int):
                eng.nop(nofuse=True)

    def repeat(eng, n, body, start=0):
        body(start)
        with eng.Fori(start + 1, n) as i:
            body(i)

    def load8(eng, regs, table, at):
        eng.load(regs, table[0:1, ds(at, 8)])
        return [eng.snap(r, min_val=0, max_val=BLOCKS - 1) for r in regs]

    def dram(name, shape, dt):
        return nc.dram_tensor(name, shape, dt, kind="Internal").ap()

    k_tab = dram("k_tab", (BLOCKS * P, D), f32)
    v_tab = dram("v_tab", (RL * P, D), f32)
    inv_d = dram("inv_d", (TROWS * P,), bf16)
    seg_d = dram("seg_d", (TROWS * P,), bf16)
    loc_d = dram("loc_d", (TROWS * P,), bf16)
    blk_d = dram("blk_d", (TROWS,), i32)

    with ctx:
        R = sb("R", [P, BLOCKS * W])
        E = sb("E", [P, (RL + 1) * P])
        wq = sb("wq", [P, KC, D])
        wv = sb("wv", [P, KC, D])
        w1 = sb("w1", [P, KC, DFF])
        w2 = sb("w2", [P, FC, D])
        ring = sb("ring", [P, RING, D])
        prod = sb("prod", [P, 4, D])
        oh = sb("oh", [P, 2, 8, P])
        loc = sb("loc", [P, 2, 8 * P], bf16)
        xt = sb("xt", [P, 2, KC, P])
        vout = sb("vout", [P, D])
        src_t = sb("src_t", [P, TROWS], i32)
        loc_t = sb("loc_t", [P, TROWS])
        blk1 = sb("blk1", [1, STEPS], i32)
        blk3 = sb("blk3", [1, STEPS], i32)
        idx = sb("idx", [P, 2, 8], i32)
        ident = sb("ident", [P, P])
        iota_row = sb("iota_row", [P, P])
        iota_col = sb("iota_col", [P, 1])
        one = sb("one", [1, 1])
        b1_col = sb("b1_col", [P, FC])
        est = sb("est", [P, HEADS, UN])
        junk = sb("junk", [P, DK])

        q_blk = R[:, :].rearrange("p (b w) -> p b w", w=W)
        wk = ring[:, 0:KC, :]
        e_all = E[:, 0:HEADS * STEPS].rearrange("p (h s) -> p h s", h=HEADS)

        s_w, s_w2, s_pc = sem("qk_weights_in"), sem("weights_in"), sem("pool_constants")
        s_x = [sem(f"xt_in{i}") for i in range(2)]
        s_qps, s_kps = sem("q_product_done"), sem("k_product_done")
        s_qout, s_kout = sem("q_copied"), sem("k_copied")
        s_kst = [sem(f"k_stored{i}") for i in range(2)]
        s_tin, s_const, s_tab = sem("table_inputs_in"), sem("constants_ready"), sem("tables_done")
        s_tidx, s_tg = sem("tile_index_ready"), sem("edge_rows_in")
        s_tT, s_tTc = sem("table_transposed"), sem("table_copied")
        s_rows, s_tst, s_tld = sem("table_rows_ready"), sem("table_rows_stored"), sem("block_rows_in")
        s_dc = sem("vector_chain")
        chain = [0]

        def link(dve, ins):
            chain[0] += 1
            ins.then_inc(s_dc, 1)
            dve.wait_ge(s_dc, chain[0])

        TB = 34 * W
        N3 = GROUPS * P

        def tmp(n, cols=N3):
            return R[:, TB + n * N3:TB + n * N3 + cols]

        last_i, lastf, key = (E[:, i * TILES:(i + 1) * TILES] for i in range(3))
        rows_i = tmp(0, 3 * N3).bitcast(i32).rearrange("p (g w) -> p g w", g=GROUPS)
        dstf = tmp(3).rearrange("p (g w) -> p g w", g=GROUPS)
        prevf = tmp(4).rearrange("p (g w) -> p g w", g=GROUPS)
        srcf = tmp(5).rearrange("p (g w) -> p g w", g=GROUPS)
        valid = tmp(6).rearrange("p (g w) -> p g w", g=GROUPS)
        packed = tmp(7, 3 * N3 // 2).bitcast(bf16).rearrange("p (k g w) -> p k g w", k=3, g=GROUPS)
        small = E[:, 3 * TILES:3 * TILES + 64]
        scol, tstep, bstep, base = (small[:, i * 8:i * 8 + GROUPS] for i in range(4))
        scol_i, tstep_i, bstep_i = (small[:, 32 + i * 8:32 + i * 8 + GROUPS].bitcast(i32) for i in range(3))
        iota_t = E[:, 4 * TILES:5 * TILES]
        iota_ti = E[:, 5 * TILES:6 * TILES].bitcast(i32)
        iota_ri = E[:, 6 * TILES:6 * TILES + P].bitcast(i32)
        iota_ci = E[:, 6 * TILES + P:6 * TILES + P + 1].bitcast(i32)


        kout = prod[:, 0:2, :]
        x_tile = lambda t: a["xt"][ds(t, 1)].rearrange("a p k n -> p (a k) n")


        kout = prod[:, 0:2, :]
        x_tile = lambda t: a["xt"][ds(t, 1)].rearrange("a p k n -> p (a k) n")

        with nc.psum_tensor("ps_q", [P, 2, D], f32) as ps_q, \
                nc.psum_tensor("ps_k", [P, 2, D], f32) as ps_k, \
                nc.psum_tensor("ps_t", [P, 2, D], f32) as ps_t, nc.Block() as block:

            @block.sync
            def _(sp):
                sp.dma_start(last_i.bitcast(i32), a["tile_last"][0:1, :].to_broadcast([P, TILES])).then_inc(s_tin, 16)
                sp.dma_start(wq[:], a["wq"]).then_inc(s_w, 16)
                sp.dma_start(wk, a["wk"]).then_inc(s_w, 16)
                sp.dma_start(wv[:], a["wv"]).then_inc(s_w2, 16)
                sp.dma_start(w1[:], a["w1"]).then_inc(s_w2, 16)
                sp.dma_start(w2[:], a["w2"]).then_inc(s_w2, 16)

                def load(t, slot):
                    wait(sp, s_kps, t - 1)
                    sp.dma_start(xt[:, slot], x_tile(t)).then_inc(s_x[slot], 16)

                def store(t, slot):
                    wait(sp, s_kout, t + 1)
                    sp.dma_start(k_tab[ds(t * P, P), :], kout[:, slot]).then_inc(s_kst[slot], 16)

                def pair(i):
                    for slot in range(2):
                        t = 2 * i + slot
                        load(t, slot)
                        if not (isinstance(t, int) and t == 0):
                            store(t - 1, 1 - slot)

                pair(0)
                with sp.Fori(1, 8) as i:
                    pair(i)
                sp.wait_ge(s_rows, 1)
                for n, t in enumerate((inv_d, seg_d, loc_d)):
                    sp.dma_start(t.rearrange("(g p w) -> p g w", p=P, w=P), packed[:, n]).then_inc(s_tst, 16)
                with nc.allow_non_contiguous_dma(reason="896 block numbers, once"):
                    sp.dma_start(blk_d.rearrange("(g p) -> p g", p=P), bstep_i).then_inc(s_tst, 16)
                    sp.wait_ge(s_tst, 64)
                    sp.dma_start(blk1[:], blk_d[0:STEPS].rearrange("(a s) -> a s", a=1)).then_inc(s_tld, 16)
                    sp.dma_start(blk3[:].rearrange("a (c j) -> a c j", j=RUNS),
                                 blk_d[0:STEPS].rearrange("(a j c) -> a c j", a=1, j=RUNS)).then_inc(s_tld, 16)
                with sp.Fori(8, BLOCKS // 2) as i:
                    pair(i)
                load(BLOCKS - 1, 0)
                store(BLOCKS - 2, 1)
                store(BLOCKS - 1, 0)
                sp.wait_ge(s_w2, 48)
                sp.wait_ge(s_tld, 32)
                sp.wait_ge(s_kst[0], 16 * (BLOCKS // 2 + 1))
                sp.wait_ge(s_kst[1], 16 * (BLOCKS // 2))

            @block.tensor
            def _(pe):
                pe.wait_ge(s_w, 32)

                def tile(i, slot):
                    t = 2 * i + slot
                    wait(pe, s_x[slot], 16 * (i + 1))
                    wait(pe, s_qout, t - 1)
                    wait(pe, s_kout, t - 1)
                    for ps, w, done in ((ps_q, wq, s_qps), (ps_k, wk, s_kps)):
                        for c in range(KC):
                            last = nc.tensor.matmul(ps[:, slot, :], xt[:, slot, c, :], w[:, c, :],
                                                    start=(c == 0), stop=(c == KC - 1))
                        last.then_inc(done, 1)

                def pair(i):
                    tile(i, 0)
                    tile(i, 1)

                pair(0)
                with pe.Fori(1, 8) as i:
                    pair(i)
                pe.wait_ge(s_const, 1)
                pe.wait_ge(s_rows, 1)
                for g in range(GROUPS):
                    for n, what in ((0, srcf), (1, dstf)):
                        wait(pe, s_tTc, 2 * g + n - 1)
                        nc.tensor.transpose(ps_t[:, n, 0:P], what[:, g, :], ident[:]).then_inc(s_tT, 1)
                with pe.Fori(8, BLOCKS // 2) as i:
                    pair(i)
                tile(BLOCKS // 2, 0)

            @block.scalar
            def _(act):
                def tile(i, slot):
                    t = 2 * i + slot
                    wait(act, s_qps, t + 1)
                    nc.scalar.activation(q_blk[:, ds(t, 1), 0:D].rearrange("p a w -> p (a w)"),
                                         ps_q[:, slot, :], ACT.Copy).then_inc(s_qout, 1)
                    wait(act, s_kps, t + 1)
                    wait(act, s_kst[slot], 16 * i)
                    nc.scalar.activation(kout[:, slot, :], ps_k[:, slot, :], ACT.Copy).then_inc(s_kout, 1)

                def pair(i):
                    tile(i, 0)
                    tile(i, 1)

                pair(0)
                with act.Fori(1, 12) as i:
                    pair(i)
                act.wait_ge(s_tTc, 2 * GROUPS)
                act.wait_ge(s_tst, 64)
                with act.Fori(12, BLOCKS // 2) as i:
                    pair(i)
                tile(BLOCKS // 2, 0)

            @block.gpsimd
            def _(pool):
                nc.gpsimd.memset(ident[:], 0.0).then_inc(s_pc, 1)
                nc.gpsimd.iota(iota_ti, [[1, TILES]], base=0, channel_multiplier=0).then_inc(s_pc, 1)
                nc.gpsimd.iota(scol_i, [[P, GROUPS]], base=0, channel_multiplier=1).then_inc(s_pc, 1)
                nc.gpsimd.iota(iota_ri, [[1, P]], base=0, channel_multiplier=0).then_inc(s_pc, 1)
                nc.gpsimd.iota(iota_ci, [[0, 1]], base=0, channel_multiplier=1).then_inc(s_pc, 1)
                nc.gpsimd.memset(one[:], 1.0).then_inc(s_pc, 1)
                pool.wait_ge(s_pc, 1)
                nc.gpsimd.affine_select(out=ident[:], in_=ident[:], compare_op=ALU.not_equal, fill=1.0,
                                        base=0, pattern=[[-1, P]], channel_multiplier=1).then_inc(s_const, 1)
                pool.wait_ge(s_tidx, 1)
                for g in range(GROUPS):
                    pool.indirect_dma_start(out=rows_i[:, g, :], out_offset=None, in_=a["edges"],
                                            in_offset=bass.IndirectOffsetOnAxis(ap=tstep_i[:, g:g + 1], axis=0),
                                            bounds_check=TILES - 1, oob_is_err=False).then_inc(s_tg, 16)
                pool.wait_ge(s_tg, 16 * GROUPS)

            @block.vector
            def _(dve):
                v = nc.vector
                dve.wait_ge(s_tin, 16)
                dve.wait_ge(s_pc, 6)
                v.tensor_copy(iota_row[:], iota_ri)
                v.tensor_copy(iota_col[:], iota_ci)
                v.tensor_copy(scol, scol_i)
                v.tensor_copy(iota_t, iota_ti)
                link(dve, v.tensor_single_scalar(last_i.bitcast(i32), last_i.bitcast(i32), 7, ALU.arith_shift_right))
                link(dve, v.tensor_copy(lastf, last_i.bitcast(i32)))
                link(dve, v.tensor_tensor(key, lastf, iota_t, ALU.add))
                for g in range(GROUPS):
                    link(dve, v.tensor_scalar(lastf, key, scol[:, g:g + 1], 0.0, ALU.is_lt, ALU.add,
                                              accum_out=tstep[:, g:g + 1]))
                link(dve, v.tensor_scalar_min(tstep, tstep, float(TILES - 1)))
                v.tensor_copy(tstep_i, tstep).then_inc(s_tidx, 1)
                link(dve, v.tensor_tensor(bstep, scol, tstep, ALU.subtract))
                link(dve, v.tensor_copy(bstep_i, bstep))
                link(dve, v.tensor_scalar_mul(base, bstep, float(P)))
                dve.wait_ge(s_tg, 16 * GROUPS)
                v.tensor_copy(srcf, rows_i[:, :, 0:P])
                v.tensor_copy(prevf, rows_i[:, :, 2 * P:3 * P])
                link(dve, v.tensor_copy(dstf, rows_i[:, :, P:2 * P]))
                link(dve, v.tensor_tensor(prevf, dstf, prevf, ALU.not_equal))
                for g in range(GROUPS):
                    ins = v.tensor_scalar(dstf[:, g, :], dstf[:, g, :], base[:, g:g + 1], None, ALU.subtract)
                link(dve, ins)
                link(dve, v.tensor_scalar(valid, dstf, 0.0, None, ALU.is_ge))
                link(dve, v.scalar_tensor_tensor(valid, dstf, float(P - 1), valid, ALU.is_le, ALU.mult))
                v.tensor_scalar(packed[:, 0], valid, 1.0, BIG, ALU.subtract, ALU.mult)
                v.scalar_tensor_tensor(packed[:, 1], prevf, -BIG, valid, ALU.mult, ALU.mult)
                link(dve, v.scalar_tensor_tensor(dstf, dstf, -255.0, valid, ALU.add, ALU.mult))
                link(dve, v.tensor_scalar_add(dstf, dstf, 255.0))
                link(dve, v.tensor_copy(packed[:, 2], dstf))
                link(dve, v.tensor_scalar(valid, valid, -float(SKIP), float(SKIP), ALU.mult, ALU.add))
                v.tensor_tensor(srcf, srcf, valid, ALU.add).then_inc(s_rows, 1)
                for g in range(GROUPS):
                    for n, to in ((0, src_t), (1, loc_t)):
                        dve.wait_ge(s_tT, 2 * g + n + 1)
                        v.tensor_copy(to[:, g * P:(g + 1) * P], ps_t[:, n, 0:P]).then_inc(s_tTc, 1)

        s_z, s_idx = sem("ring_cleared"), sem("index_columns_ready")
        s_k = [sem(f"k_rows_in{i}") for i in range(RING)]
        s_loc = [sem(f"loc_in{i}") for i in range(2)]
        s_oh, s_qx, s_mul, s_sum = sem("onehot_ready"), sem("q_expanded"), sem("product_ready"), sem("scalar_heads_summed")
        s_red, s_xv, s_vps, s_vout, s_vst = (sem(n) for n in ("vector_heads_summed", "xt_for_v_in", "v_product_done", "v_copied", "v_stored"))
        s_mc, s_ac = sem("vector_scores_moved"), sem("scalar_scores_moved")

        def load_loc(sp, n, half):
            sp.dma_start(loc[:, half], loc_d[ds(n * 8 * P, 8 * P)].rearrange("(a w) -> a w", a=1)
                         .to_broadcast([P, 8 * P])).then_inc(s_loc[half], 16)

        with nc.psum_tensor("ps_qx", [P, 4, D], f32) as ps_qx, \
                nc.psum_tensor("ps_v", [P, D], f32) as ps_v, nc.Block() as block:

            @block.sync
            def _(sp):
                load_loc(sp, 0, 0)
                load_loc(sp, 1, 1)
                sp.dma_start(xt[:, 0], x_tile(0)).then_inc(s_xv, 16)

                def body(i):
                    for half in range(2):
                        n = 2 * i + 2 + half
                        wait(sp, s_oh, n - 1)
                        load_loc(sp, n, half)
                    wait(sp, s_vout, i + 1)
                    sp.dma_start(v_tab[ds(i * P, P), :], vout[:]).then_inc(s_vst, 16)
                    wait(sp, s_vst, 16 * (i + 1))
                    sp.dma_start(xt[:, 0], x_tile(i + 1)).then_inc(s_xv, 16)

                repeat(sp, RL, body)
                for half in range(2):
                    sp.wait_ge(s_loc[half], 16 * (RL + 1))
                sp.wait_ge(s_xv, 16 * (RL + 1))

            @block.gpsimd
            def _(pool):
                nc.gpsimd.memset(ring[:], 0.0).then_inc(s_z, 1)
                pool.wait_ge(s_z, 1)
                bound = pool.to_reg(BLOCKS * P - 1)

                def body(i):
                    for half in range(2):
                        s = UN * i + 8 * half
                        wait(pool, s_mul, s - 7)
                        nc.gpsimd.tensor_copy(idx[:, half, :], src_t[:, ds(s, 8)]).then_inc(s_idx, 1)
                        wait(pool, s_idx, 2 * i + half + 1)
                        for u in range(8):
                            wait(pool, s_mul, s + u - 7)
                            pool.indirect_dma_start(out=ring[:, u, :], out_offset=None, in_=k_tab,
                                                    in_offset=bass.IndirectOffsetOnAxis(ap=idx[:, half, u:u + 1], axis=0),
                                                    bounds_check=bound, oob_is_err=False).then_inc(s_k[u], 16)

                repeat(pool, RL, body)

            @block.tensor
            def _(pe):
                regs = [pe.alloc_register(f"pe_blk{u}") for u in range(8)]

                def body(i):
                    for half in range(2):
                        blk = load8(pe, regs, blk1, UN * i + 8 * half)
                        wait(pe, s_oh, 2 * i + half + 1)
                        for u in range(8):
                            s = UN * i + 8 * half + u
                            wait(pe, s_mul, s - 3)
                            nc.tensor.matmul(ps_qx[:, u % 4, :], oh[:, half, u, :],
                                             q_blk[:, ds(blk[u], 1), 0:D].rearrange("p a w -> p (a w)"),
                                             start=True, stop=True).then_inc(s_qx, 1)
                            if half and u % 2:
                                c = u // 2
                                if c == 0:
                                    wait(pe, s_xv, 16 * (i + 1))
                                last = nc.tensor.matmul(ps_v[:], xt[:, 0, c, :], wv[:, c, :],
                                                        start=(c == 0), stop=(c == KC - 1))
                                if c == KC - 1:
                                    last.then_inc(s_vps, 1)

                repeat(pe, RL, body)

            @block.vector
            def _(dve):
                def build(n, half):
                    wait(dve, s_loc[half], 16 * ((n - half) // 2 + 1) if isinstance(n, int) else 8 * (n - half) + 16)
                    wait(dve, s_qx, 8 * (n - 1))
                    nc.vector.tensor_scalar(oh[:, half].rearrange("p u w -> p (u w)"), loc[:, half],
                                            iota_col[:, 0:1], None, ALU.is_equal).then_inc(s_oh, 1)

                build(0, 0)

                def body(i):
                    for u in range(UN):
                        s = UN * i + u
                        if u == 4:
                            build(2 * i + 1, 1)
                        if u == 12:
                            build(2 * i + 2, 0)
                        wait(dve, s_qx, s + 1)
                        wait(dve, s_k[u % 8], 32 * i + 16 * (u // 8 + 1))
                        wait(dve, s_sum, s - 3)
                        nc.vector.tensor_tensor(prod[:, u % 4, :], ps_qx[:, u % 4, :], ring[:, u % 8, :],
                                                ALU.mult).then_inc(s_mul, 1)
                        if u:
                            sums(s - 1, u - 1)
                    sums(UN * i + UN - 1, UN - 1)
                    wait(dve, s_red, UN * i + UN)
                    nc.vector.tensor_copy(e_all[:, 0:DVH, ds(UN * i, UN)], est[:, 0:DVH, :]).then_inc(s_mc, 1)
                    wait(dve, s_mc, i + 1)

                def sums(s, u):
                    wait(dve, s_mul, s + 1)
                    nc.vector.tensor_reduce(est[:, 0:DVH, u], prod[:, u % 4, 0:DVH * DK]
                                            .rearrange("p (h d) -> p h d", h=DVH), AX.X, ALU.add).then_inc(s_red, 1)

                repeat(dve, RL, body)

            @block.scalar
            def _(act):
                def body(i):
                    for u in range(UN):
                        s = UN * i + u
                        wait(act, s_mul, s + 1)
                        for h in range(DVH, HEADS):
                            part = prod[:, u % 4, h * DK:(h + 1) * DK]
                            ins = nc.scalar.activation(part, part, ACT.Copy,
                                                       accum_out=est[:, h, u:u + 1])
                        ins.then_inc(s_sum, 1)
                    wait(act, s_sum, UN * i + UN)
                    nc.scalar.activation(e_all[:, DVH:HEADS, ds(UN * i, UN)], est[:, DVH:HEADS, :], ACT.Copy).then_inc(s_ac, 1)
                    wait(act, s_ac, i + 1)
                    wait(act, s_vps, i + 1)
                    nc.scalar.activation(vout[:], ps_v[:], ACT.Copy).then_inc(s_vout, 1)

                repeat(act, RL, body)

        s_mi = sem("masks_in")
        s_sc, s_eT, s_eM = sem("scores_staged"), sem("scores_transposed"), sem("scores_masked")
        s_col, s_colT, s_row, s_rowT = sem("ends_ready"), sem("ends_transposed"), sem("carries_ready"), sem("carries_transposed")
        s_dead, s_zero, s_wo = sem("maxima_work_dead"), sem("sums_cleared"), sem("late_weights_in")

        sc_t = R[:, 0:RE]
        mx_t = R[:, RE:2 * RE]
        seg_t = R[:, 2 * RE:2 * RE + RE // 2 + 2].bitcast(bf16)
        inv_t = R[:, 2 * RE + RE // 2 + 2:3 * RE + 2].bitcast(bf16)
        work_end = 3 * RE + 2
        stage = prod[:, 0:2, 0:2 * P]
        cols = est[:, 0, 0:8]
        rows = oh[0:1, 0, :, :]
        e_runs = e_all.rearrange("p h (j c) -> p c h j", c=RL)
        gains = [wv[:, c, :] for c in range(4)] + [vout[:]]

        with nc.psum_tensor("ps_e", [P, 2, D], f32) as ps_e, \
                nc.psum_tensor("ps_c", [P, 2, D], f32) as ps_c, nc.Block() as block:

            @block.sync
            def _(sp):
                for h in range(HEADS):
                    at = slice(h * RUNS, (h + 1) * RUNS)
                    sp.dma_start(inv_t[at, 0:RE], inv_d[0:RUNS * RE].rearrange("(j w) -> j w", j=RUNS)).then_inc(s_mi, 16)
                    sp.dma_start(seg_t[at, 0:RE], seg_d[0:RUNS * RE].rearrange("(j w) -> j w", j=RUNS)).then_inc(s_mi, 16)
                    with nc.allow_non_contiguous_dma(reason="the first slot of the next run, 16 values"):
                        sp.dma_start(seg_t[at, RE:RE + 1], seg_d[RE:(RUNS + 1) * RE].rearrange("(j w) -> j w", j=RUNS)[:, 0:1]).then_inc(s_mi, 16)
                sp.dma_start(wq[:], a["wo"]).then_inc(s_wo, 16)
                for name, to in zip(("ln1_g", "ln1_b", "ln2_g", "ln2_b", "b2"), gains):
                    sp.dma_start(to, a[name].to_broadcast([P, D])).then_inc(s_wo, 16)
                sp.dma_start(b1_col[:], a["b1"]).then_inc(s_wo, 16)
                sp.wait_ge(s_mi, 16 * 3 * HEADS)
                sp.wait_ge(s_wo, 16 * 7)

            @block.scalar
            def _(act):
                def body(i):
                    for slot in range(2):
                        n = 2 * i + slot
                        wait(act, s_eT, n - 1)
                        nc.scalar.activation(stage[:, slot, :].rearrange("p (c h j) -> p c h j", c=2, h=HEADS),
                                             e_runs[:, ds(2 * n, 2), :, :], ACT.Copy).then_inc(s_sc, 1)

                repeat(act, RL // 4, body)

            @block.tensor
            def _(pe):
                def body(i):
                    for slot in range(2):
                        n = 2 * i + slot
                        wait(pe, s_sc, n + 1)
                        wait(pe, s_eM, n - 1)
                        for c in range(2):
                            ins = nc.tensor.transpose(ps_e[:, slot, c * P:(c + 1) * P],
                                                      stage[:, slot, c * P:(c + 1) * P], ident[:])
                        ins.then_inc(s_eT, 1)

                repeat(pe, RL // 4, body)
                for way in range(2):
                    pe.wait_ge(s_col, way + 1)
                    for n in range(2):
                        ins = nc.tensor.transpose(ps_c[0:1, 0, n * P:(n + 1) * P], cols[:, 2 * way + n:2 * way + n + 1], ident[:])
                    ins.then_inc(s_colT, 1)
                    pe.wait_ge(s_row, way + 1)
                    nc.tensor.matmul(ps_c[:, 1, 0:1], rows[0:1, 4 * way + 3, :], one[0:1, 0:1],
                                     start=True, stop=True).then_inc(s_rowT, 1)

            @block.gpsimd
            def _(pool):
                nc.gpsimd.memset(R[:, work_end:BLOCKS * W], 0.0).then_inc(s_zero, 1)
                pool.wait_ge(s_dead, 1)
                nc.gpsimd.memset(R[:, RE + RE // 2:work_end], 0.0).then_inc(s_zero, 1)

            @block.vector
            def _(dve):
                v = nc.vector
                dve.wait_ge(s_mi, 16 * 3 * HEADS)

                def body(i):
                    for slot in range(2):
                        n = 2 * i + slot
                        wait(dve, s_eT, n + 1)
                        v.tensor_tensor(sc_t[:, ds(2 * P * n, 2 * P)], ps_e[:, slot, 0:2 * P],
                                        inv_t[:, ds(2 * P * n, 2 * P)], ALU.add).then_inc(s_eM, 1)

                repeat(dve, RL // 4, body)
                dve.wait_ge(s_eM, RL // 2)

                for way, (reset, data, to) in enumerate(((seg_t[:, 0:RE], sc_t, mx_t),
                                                         (seg_t[:, RE:0:-1], mx_t[:, ::-1], E[:, RE - 1::-1] if RE == HEADS * STEPS else None))):
                    end = RE - 1 if way == 0 else 0
                    trial = E[:, 0:RE] if way == 0 else E[:, 0:RE][:, ::-1]
                    link(dve, v.tensor_tensor_scan(trial, reset, data, -BIG, ALU.add, ALU.max))
                    v.tensor_copy(cols[:, 2 * way:2 * way + 1], E[:, end:end + 1])
                    v.tensor_reduce(cols[:, 2 * way + 1:2 * way + 2], reset, AX.X, ALU.min).then_inc(s_col, 1)
                    dve.wait_ge(s_colT, way + 1)
                    got, res, inc, carry = (rows[0:1, 4 * way + n, :] for n in range(4))
                    heads = lambda r: r.rearrange("a (h j) -> a h j", h=HEADS)
                    v.tensor_copy(got, ps_c[0:1, 0, 0:P])
                    link(dve, v.tensor_copy(res, ps_c[0:1, 0, P:2 * P]))
                    first = 0 if way == 0 else RUNS - 1
                    v.memset(carry, -BIG)
                    link(dve, v.memset(heads(res)[:, :, first:first + 1], -BIG))
                    if way == 0:
                        link(dve, v.tensor_tensor_scan(inc, res, got, -BIG, ALU.add, ALU.max))
                        v.tensor_copy(heads(carry)[:, :, 1:RUNS], heads(inc)[:, :, 0:RUNS - 1]).then_inc(s_row, 1)
                    else:
                        link(dve, v.tensor_tensor_scan(inc[:, ::-1], res[:, ::-1], got[:, ::-1], -BIG, ALU.add, ALU.max))
                        v.tensor_copy(heads(carry)[:, :, 0:RUNS - 1], heads(inc)[:, :, 1:RUNS]).then_inc(s_row, 1)
                    dve.wait_ge(s_rowT, way + 1)
                    link(dve, v.tensor_copy(cols[:, 4 + way:5 + way], ps_c[:, 1, 0:1]))
                    link(dve, v.tensor_tensor_scan(mx_t if way == 0 else mx_t[:, ::-1], reset, data,
                                                   cols[:, 4 + way:5 + way], ALU.add, ALU.max))
                v.memset(E[:, RE:RE + P], 0.0)
                v.tensor_tensor(E[:, 0:RE], sc_t, mx_t, ALU.subtract).then_inc(s_dead, 1)
                dve.wait_ge(s_dead, 1)
                v.memset(R[:, 0:RE + RE // 2], 0.0).then_inc(s_zero, 1)

        s_v = [sem(f"v_rows_in{i}") for i in range(RING)]
        s_idx3, s_loc3, s_oh3 = sem("v_index_columns_ready"), sem("loc_columns_ready"), sem("v_onehot_ready")
        s_exp, s_exT, s_exc = sem("weights_ready"), sem("weights_transposed"), sem("weights_copied")
        s_wd, s_wa, s_pv, s_acc = sem("vector_heads_weighted"), sem("scalar_heads_weighted"), sem("step_summed"), sem("step_added")
        src_c = src_t[:, 0:STEPS].rearrange("p (j c) -> p c j", c=RL)
        loc_c = loc_t[:, 0:STEPS].rearrange("p (j c) -> p c j", c=RL)
        oht = oh[:, 0, 0:4, :]
        exs = oh[:, 0, 4:6, :]
        exl = oh[:, 0, 6:8, :]
        locr = est[:, 0:2, :]

        with nc.psum_tensor("ps_a", [P, 2, 2 * D], f32) as ps_a, \
                nc.psum_tensor("ps_ex", [P, 2, D], f32) as ps_ex, nc.Block() as block:

            @block.gpsimd
            def _(pool):
                bound = pool.to_reg(BLOCKS * P - 1)

                def body(i):
                    for q in range(4):
                        par, half = divmod(q, 2)
                        s = 2 * UN * i + 8 * q
                        wait(pool, s_wd, s - 7)
                        wait(pool, s_wa, s - 7)
                        nc.gpsimd.tensor_copy(idx[:, half, :], src_c[:, ds(2 * i + par, 1), 8 * half:8 * half + 8]
                                              .rearrange("p c j -> p (c j)")).then_inc(s_idx3, 1)
                        wait(pool, s_idx3, 4 * i + q + 1)
                        for u in range(8):
                            wait(pool, s_wd, s + u - 7)
                            wait(pool, s_wa, s + u - 7)
                            pool.indirect_dma_start(out=ring[:, u, :], out_offset=None, in_=v_tab,
                                                    in_offset=bass.IndirectOffsetOnAxis(ap=idx[:, half, u:u + 1], axis=0),
                                                    bounds_check=bound, oob_is_err=False).then_inc(s_v[u], 16)

                repeat(pool, RL // 2, body)

            @block.scalar
            def _(act):
                def weights(c, slot):
                    wait(act, s_exT, c - 1)
                    nc.scalar.activation(exs[:, slot, :], E[:, ds(c * P, P)], ACT.Exp, scale=DK ** -0.5).then_inc(s_exp, 1)

                def copies(c, slot):
                    wait(act, s_exT, c + 1)
                    wait(act, s_pv, UN * (c - 1))
                    nc.scalar.activation(exl[:, slot, :], ps_ex[:, slot, 0:P], ACT.Copy).then_inc(s_exc, 1)

                weights(0, 0)
                copies(0, 0)

                def body(i):
                    for par in range(2):
                        c = 2 * i + par
                        for j in range(UN):
                            s = UN * c + j
                            if j == 6:
                                weights(c + 1, 1 - par)
                            if j == 12:
                                copies(c + 1, 1 - par)
                            if j == 0:
                                wait(act, s_exc, c + 1)
                            wait(act, s_v[j % 8], 32 * c + 16 * (j // 8 + 1))
                            wait(act, s_pv, s - 3)
                            for h in range(DVH, HEADS):
                                ins = nc.scalar.activation(prod[:, j % 4, h * DK:(h + 1) * DK],
                                                           ring[:, j % 8, h * DK:(h + 1) * DK], ACT.Copy,
                                                           scale=exl[:, par, h * RUNS + j:h * RUNS + j + 1])
                            ins.then_inc(s_wa, 1)

                repeat(act, RL // 2, body)

            @block.tensor
            def _(pe):
                def turn(c, slot):
                    wait(pe, s_exp, c + 1)
                    wait(pe, s_wd, UN * (c - 1))
                    wait(pe, s_exc, c - 1)
                    nc.tensor.transpose(ps_ex[:, slot, 0:P], exs[:, slot, :], ident[:]).then_inc(s_exT, 1)

                turn(0, 0)

                def body(i):
                    for par in range(2):
                        c = 2 * i + par
                        for j in range(UN):
                            s = UN * c + j
                            if j == 10:
                                turn(c + 1, 1 - par)
                            if j == 0:
                                wait(pe, s_exc, c + 1)
                            wait(pe, s_oh3, s + 1)
                            wait(pe, s_wd, s + 1)
                            wait(pe, s_wa, s + 1)
                            wait(pe, s_acc, s - 1)
                            nc.tensor.matmul(ps_a[:, j % 2, 0:D], oht[:, j % 4, :], prod[:, j % 4, :],
                                             start=True, stop=True)
                            nc.tensor.matmul(ps_a[:, j % 2, D:W], oht[:, j % 4, :],
                                             exl[:, par, :].rearrange("p (h j) -> p h j", h=HEADS)[:, :, j],
                                             start=True, stop=True).then_inc(s_pv, 1)

                repeat(pe, RL // 2, body)

            @block.vector
            def _(dve):
                v = nc.vector
                regs = [dve.alloc_register(f"dve_blk{u}") for u in range(8)]
                dve.wait_ge(s_zero, 3)
                blk = {}

                def add(i, n):
                    s = 2 * UN * i + n
                    if n % 8 == 0:
                        blk[0] = load8(dve, regs, blk3, s)
                    to = q_blk[:, ds(blk[0][n % 8], 1), :].rearrange("p a w -> p (a w)")
                    wait(dve, s_pv, s + 1)
                    wait(dve, s_acc, s)
                    v.tensor_tensor(to, to, ps_a[:, n % 2, 0:W], ALU.add).then_inc(s_acc, 1)

                def body(i):
                    for par in range(2):
                        c = 2 * i + par
                        wait(dve, s_oh3, UN * (c - 1))
                        v.tensor_copy(locr[:, par, :], loc_c[:, ds(c, 1), :].rearrange("p c j -> p (c j)")).then_inc(s_loc3, 1)
                        wait(dve, s_loc3, c + 1)
                        for j in range(UN):
                            s = UN * c + j
                            wait(dve, s_pv, s - 3)
                            v.tensor_scalar(oht[:, j % 4, :], iota_row[:], locr[:, par, j:j + 1], None,
                                            ALU.is_equal).then_inc(s_oh3, 1)
                            wait(dve, s_exc, c + 1)
                            wait(dve, s_v[j % 8], 32 * c + 16 * (j // 8 + 1))
                            v.tensor_tensor(prod[:, j % 4, 0:DVH * DK].rearrange("p (h d) -> p h d", h=DVH),
                                            ring[:, j % 8, 0:DVH * DK].rearrange("p (h d) -> p h d", h=DVH),
                                            ps_ex[:, par, 0:P].rearrange("p (h j) -> p h j", h=HEADS)[:, 0:DVH, j:j + 1]
                                            .to_broadcast([P, DVH, DK]), ALU.mult).then_inc(s_wd, 1)
                            if UN * par + j >= 2:
                                add(i, UN * par + j - 2)
                    add(i, 2 * UN - 2)
                    add(i, 2 * UN - 1)

                repeat(dve, RL // 2, body)

        s_xa = [sem(f"x_for_residual1_in{i}") for i in range(2)]
        s_xb = [sem(f"x_for_residual2_in{i}") for i in range(2)]
        s_st = [sem(f"out_stored{i}") for i in range(2)]
        names = ("rz", "an", "aT", "aTc", "o", "t1", "mv1", "sd1", "rs1", "n1", "x1", "x1b", "xT", "xTc",
                 "h", "hr", "f", "t2", "mv2", "sd2", "rs2", "n2", "y", "mv3", "sd3", "fin")
        (f_rz, f_an, f_aT, f_aTc, f_o, f_t1, f_mv1, f_sd1, f_rs1, f_n1, f_x1, f_x1b, f_xT, f_xTc,
         f_h, f_hr, f_f, f_t2, f_mv2, f_sd2, f_rs2, f_n2, f_y, f_mv3, f_sd3, f_fin) = (sem("finish_" + n) for n in names)
        f_z, f_g1, f_g2, f_o2, f_nm3 = (sem("finish_" + n) for n in ("z", "g1", "g2", "o2", "nm3"))
        f_bs = [sem(f"finish_bn_stats{n}") for n in range(3)]
        f_rc = [sem(f"finish_reciprocal{n}") for n in range(3)]

        def pairs(k):
            return [E[:, (2 * k + n) * D:(2 * k + n + 1) * D] for n in range(2)]

        an, aT, x1, x1T, x1b, t2 = (pairs(k) for k in range(6))
        xa, xb, outb = ([ring[:, 2 * k + n, :] for n in range(2)] for k in range(3))
        hT = [oh[:, 0, 2 * n:2 * n + 2, :].rearrange("p a w -> p (a w)") for n in range(2)]
        g1, o1, g2, o2, b2 = gains
        wo = wq
        zr = est[:, 0:2, 0:HEADS]
        stat = [[est[:, 2 + ln * 2 + n, :] for n in range(2)] for ln in range(3)]
        eps = est[:, 1, 15:16]
        in_range = lambda t: not isinstance(t, int) or 0 <= t < BLOCKS

        with ExitStack() as banks, nc.Block() as block:
            pb = lambda name: banks.enter_context(nc.psum_tensor(name, [P, D], f32))
            ps_aT, ps_o, ps_xT, ps_h, ps_f = (pb(n) for n in ("ps_aT", "ps_o", "ps_xT", "ps_h", "ps_f"))

            def run(eng, period):
                for k in range(-1, 4):
                    period(k, k % 2)
                with eng.Fori(2, BLOCKS // 2) as i:
                    period(2 * i, 0)
                    period(2 * i + 1, 1)
                for k in range(BLOCKS - 1, BLOCKS + 2):
                    period(k, k % 2)

            @block.sync
            def _(sp):
                def period(k, slot):
                    t = k + 1
                    if in_range(t):
                        p = 1 - slot
                        wait(sp, f_t1, t - 1)
                        sp.dma_start(xa[p], a["x"][ds(t * P, P), :]).then_inc(s_xa[p], 16)
                    t = k - 1
                    if in_range(t):
                        p = 1 - slot
                        wait(sp, f_y, t - 1)
                        sp.dma_start(xb[p], a["x"][ds(t * P, P), :]).then_inc(s_xb[p], 16)
                    t = k - 3
                    if in_range(t):
                        store(t, 1 - slot, P)

                def store(t, p, n):
                    wait(sp, f_fin, t + 1)
                    sp.dma_start(out[ds(t * P, n), :], outb[p][0:n, :]).then_inc(s_st[p], 16)

                run(sp, period)
                store(BLOCKS - 1, 0, NODES - (BLOCKS - 1) * P)
                sp.wait_ge(s_st[0], 16 * (BLOCKS // 2 + 1))
                sp.wait_ge(s_st[1], 16 * (BLOCKS // 2))

            @block.tensor
            def _(pe):
                def period(k, slot):
                    if in_range(k):
                        wait(pe, f_an, k + 1)
                        wait(pe, f_aTc, k)
                        for c in range(KC):
                            ins = nc.tensor.transpose(ps_aT[:, c * P:(c + 1) * P], an[slot][:, c * P:(c + 1) * P], ident[:])
                        ins.then_inc(f_aT, 1)
                        wait(pe, f_aTc, k + 1)
                        wait(pe, f_t1, k)
                        for c in range(KC):
                            ins = nc.tensor.matmul(ps_o[:], aT[slot][:, c * P:(c + 1) * P], wo[:, c, :],
                                                   start=(c == 0), stop=(c == KC - 1))
                        ins.then_inc(f_o, 1)
                    t, p = k - 1, 1 - slot
                    if in_range(t):
                        wait(pe, f_x1, t + 1)
                        wait(pe, f_xTc, t)
                        for c in range(KC):
                            ins = nc.tensor.transpose(ps_xT[:, c * P:(c + 1) * P], x1[p][:, c * P:(c + 1) * P], ident[:])
                        ins.then_inc(f_xT, 1)
                        wait(pe, f_xTc, t + 1)
                        wait(pe, f_hr, t)
                        for j in range(FC):
                            for c in range(KC):
                                ins = nc.tensor.matmul(ps_h[:, j * P:(j + 1) * P], w1[:, c, j * P:(j + 1) * P],
                                                       x1T[p][:, c * P:(c + 1) * P], start=(c == 0), stop=(c == KC - 1))
                        ins.then_inc(f_h, 1)
                        wait(pe, f_hr, t + 1)
                        wait(pe, f_t2, t)
                        for j in range(FC):
                            ins = nc.tensor.matmul(ps_f[:], hT[p][:, j * P:(j + 1) * P], w2[:, j, :],
                                                   start=(j == 0), stop=(j == FC - 1))
                        ins.then_inc(f_f, 1)

                run(pe, period)

            @block.scalar
            def _(act):
                def root(s, src, done, n):
                    wait(act, src, n)
                    nc.scalar.activation(s[:, 8:9], s[:, 7:8], ACT.Sqrt, bias=eps).then_inc(done, 1)

                def norm(s, x, src, done, n):
                    wait(act, src, n)
                    nc.scalar.activation(x, x, ACT.Identity, scale=s[:, 9:10], bias=s[:, 10:11]).then_inc(done, 1)

                def period(k, slot):
                    t, p = k, slot
                    if in_range(t):
                        wait(act, f_aT, t + 1)
                        wait(act, f_o, t - 1)
                        nc.scalar.activation(aT[p], ps_aT[:], ACT.Copy).then_inc(f_aTc, 1)
                    t, p = k - 2, slot
                    if in_range(t):
                        root(stat[1][p], f_mv2, f_sd2, t + 1)
                        norm(stat[1][p], t2[p], f_rs2, f_n2, t + 1)
                    t, p = k - 1, 1 - slot
                    if in_range(t):
                        wait(act, f_xT, t + 1)
                        wait(act, f_h, t - 1)
                        nc.scalar.activation(x1T[p], ps_xT[:], ACT.Copy).then_inc(f_xTc, 1)
                    t, p = k, slot
                    if in_range(t):
                        root(stat[0][p], f_mv1, f_sd1, t + 1)
                        norm(stat[0][p], x1[p], f_rs1, f_n1, t + 1)
                    t, p = k - 1, 1 - slot
                    if in_range(t):
                        wait(act, f_h, t + 1)
                        wait(act, f_f, t - 1)
                        for j in range(FC):
                            ins = nc.scalar.activation(hT[p][:, j * P:(j + 1) * P], ps_h[:, j * P:(j + 1) * P],
                                                       ACT.Relu, bias=b1_col[:, j:j + 1])
                        ins.then_inc(f_hr, 1)
                    t, p = k - 2, slot
                    if in_range(t):
                        root(stat[2][p], f_mv3, f_sd3, t + 1)

                run(act, period)

            @block.gpsimd
            def _(pool):
                def period(k, slot):
                    t, p = k - 2, slot
                    if in_range(t):
                        wait(pool, f_n2, t + 1)
                        nc.gpsimd.tensor_tensor(t2[p], t2[p], g2, ALU.mult).then_inc(f_g2, 1)
                        wait(pool, f_g2, t + 1)
                        nc.gpsimd.tensor_tensor(t2[p], t2[p], o2, ALU.add).then_inc(f_o2, 1)
                        wait(pool, f_o2, t + 1)
                        wait(pool, s_xb[p], 8 * (t - p) + 16)
                        nc.gpsimd.tensor_tensor(t2[p], t2[p], xb[p], ALU.add).then_inc(f_y, 1)
                    t, p = k + 1, 1 - slot
                    if in_range(t):
                        wait(pool, f_rz, t + 1)
                        wait(pool, f_aT, t - 1)
                        nc.gpsimd.tensor_tensor(an[p].rearrange("p (h d) -> p h d", h=HEADS),
                                                q_blk[:, ds(t, 1), 0:D].rearrange("p a (h d) -> p (a h) d", h=HEADS),
                                                zr[:, p, :].unsqueeze(2).to_broadcast([P, HEADS, DK]), ALU.mult).then_inc(f_an, 1)
                    t, p = k, slot
                    if in_range(t):
                        wait(pool, f_n1, t + 1)
                        nc.gpsimd.tensor_tensor(x1[p], x1[p], g1, ALU.mult).then_inc(f_g1, 1)
                        wait(pool, f_g1, t + 1)
                        nc.gpsimd.tensor_tensor(x1[p], x1[p], o1, ALU.add).then_inc(f_x1, 1)

                run(pool, period)

            @block.vector
            def _(dve):
                v = nc.vector
                v.memset(eps, EPS)

                def stats(ln, p, x, ready, n, done):
                    s = stat[ln][p]
                    wait(dve, ready, n)
                    v.bn_stats(s[:, 0:6], x).then_inc(f_bs[ln], 1)
                    wait(dve, f_bs[ln], n)
                    dve.nop(nofuse=True)
                    v.bn_aggr(s[:, 6:8], s[:, 0:6]).then_inc(done, 1)

                def scales(ln, p, ready, n, done):
                    s = stat[ln][p]
                    wait(dve, ready, n)
                    v.reciprocal(s[:, 9:10], s[:, 8:9]).then_inc(f_rc[ln], 1)
                    wait(dve, f_rc[ln], n)
                    v.tensor_scalar(s[:, 10:11], s[:, 6:7], s[:, 9:10], -1.0, ALU.mult, ALU.mult).then_inc(done, 1)

                def period(k, slot):
                    t, p = k - 2, slot
                    if in_range(t):
                        wait(dve, f_f, t + 1)
                        wait(dve, f_x1b, t + 1)
                        v.tensor_tensor(t2[p], ps_f[:], x1b[p], ALU.add).then_inc(f_t2, 1)
                        stats(1, p, t2[p], f_t2, t + 1, f_mv2)
                    t, p = k + 1, 1 - slot
                    if in_range(t):
                        wait(dve, f_an, t - 1)
                        z = q_blk[:, ds(t, 1), D:W].rearrange("p a w -> p (a w)")
                        v.tensor_scalar_max(zr[:, p, :], z, 1e-30).then_inc(f_z, 1)
                        wait(dve, f_z, t + 1)
                        v.reciprocal(zr[:, p, :], zr[:, p, :]).then_inc(f_rz, 1)
                    t, p = k - 2, slot
                    if in_range(t):
                        scales(1, p, f_sd2, t + 1, f_rs2)
                    t, p = k - 1, 1 - slot
                    if in_range(t):
                        wait(dve, f_x1, t + 1)
                        v.tensor_tensor(x1b[p], x1[p], b2, ALU.add).then_inc(f_x1b, 1)
                    t, p = k, slot
                    if in_range(t):
                        wait(dve, f_o, t + 1)
                        wait(dve, s_xa[p], 8 * (t - p) + 16)
                        v.tensor_tensor(x1[p], ps_o[:], xa[p], ALU.add).then_inc(f_t1, 1)
                        stats(0, p, x1[p], f_t1, t + 1, f_mv1)
                        scales(0, p, f_sd1, t + 1, f_rs1)
                    t, p = k - 2, slot
                    if in_range(t):
                        stats(2, p, t2[p], f_y, t + 1, f_mv3)
                        scales(2, p, f_sd3, t + 1, f_nm3)
                        wait(dve, f_nm3, t + 1)
                        wait(dve, s_st[p], 8 * (t - p))
                        v.tensor_scalar(outb[p], t2[p], stat[2][p][:, 9:10], stat[2][p][:, 10:11],
                                        ALU.mult, ALU.add).then_inc(f_fin, 1)

                run(dve, period)


def kernel(**inputs):
    import numpy as np
    import concourse.bacc as bacc
    from concourse.bass_utils import run_bass_kernel_spmd

    g = {k.replace("L0_gnn_", ""): np.asarray(v) for k, v in inputs.items()}
    x = np.zeros((XT * P, D), g["x"].dtype)
    x[:NODES] = g["x"]
    n = TILES * P
    edges = np.zeros((3, n), g["src"].dtype)
    edges[0, :EDGES] = g["src"]
    edges[1, :] = BLOCKS * P - 1
    edges[1, :EDGES] = g["dst"]
    edges[2, 0] = -1
    edges[2, 1:] = edges[1, :-1]
    arrays = {
        "x": x,
        "xt": np.ascontiguousarray(x.reshape(XT, P, KC, P).transpose(0, 3, 2, 1)),
        "edges": np.ascontiguousarray(edges.reshape(3, TILES, P).transpose(1, 0, 2)).reshape(TILES, 3 * P),
        "tile_last": np.ascontiguousarray(edges[1].reshape(TILES, P)[:, -1]).reshape(1, TILES),
        "b1": np.ascontiguousarray(g["b1"].reshape(FC, P).T),
    }
    for name in ("Wq", "Wk", "Wv", "Wo", "W1", "W2"):
        w = g[name]
        arrays[name.lower()] = np.ascontiguousarray(w.reshape(w.shape[0] // P, P, w.shape[1]).transpose(1, 0, 2))
    for name in ("ln1_g", "ln1_b", "ln2_g", "ln2_b", "b2"):
        arrays[name] = g[name].reshape(1, D)
    nc = bacc.Bacc("TRN2", target_bir_lowering=False, num_devices=1)
    aps = {k: nc.dram_tensor("in_" + k, v.shape, mybir.dt.from_np(v.dtype), kind="ExternalInput").ap()
           for k, v in arrays.items()}
    out = nc.dram_tensor("out_0", (NODES, D), mybir.dt.float32, kind="ExternalOutput").ap()
    program(nc, aps, out)
    r = run_bass_kernel_spmd(nc, [{"in_" + k: v for k, v in arrays.items()}], core_ids=[0])
    return r.results[0]["out_0"]
```

```python
import concourse.bass as bass
from concourse import mybir
from contextlib import ExitStack

P = 128
NODES, EDGES, D, HEADS, DFF = 6250, 100000, 512, 8, 256
DK = D // HEADS
KC = D // P
FC = DFF // P
BLOCKS = -(-NODES // P)
TILES = 784
STEPS = 832
UN = 16
RUNS = 16
RL = STEPS // RUNS
RE = RL * P
GROUPS = 7
TROWS = GROUPS * P
XT = 53
W = D + HEADS
RING = 8
SKIP = 20000
BIG = 2.0 ** 126
EPS = 1e-5
SUM_HEADS = 4
MUL_HEADS = 4


def program(nc, a, out):
    f32, bf16, i32 = mybir.dt.float32, mybir.dt.bfloat16, mybir.dt.int32
    ALU, ACT, AX = mybir.AluOpType, mybir.ActivationFunctionType, mybir.AxisListType
    ds = bass.ds
    ctx = ExitStack()

    def sb(name, shape, dt=f32):
        return ctx.enter_context(nc.sbuf_tensor(name, shape, dt))

    def sem(name):
        return ctx.enter_context(nc.semaphore(name))

    def wait(eng, s, n):
        if not isinstance(n, int) or n > 0:
            eng.wait_ge(s, n)
            if eng is nc.gpsimd and not isinstance(n, int):
                eng.nop(nofuse=True)

    def repeat(eng, n, body, start=0):
        body(start)
        with eng.Fori(start + 1, n) as i:
            body(i)

    def load8(eng, regs, table, at):
        eng.load(regs, table[0:1, ds(at, 8)])
        return [eng.snap(r, min_val=0, max_val=BLOCKS - 1) for r in regs]

    def wait(eng, s, n):
        if not isinstance(n, int) or n > 0:
            eng.wait_ge(s, n)
            if eng is nc.gpsimd and not isinstance(n, int):
                eng.nop(nofuse=True)

    def repeat(eng, n, body, start=0):
        body(start)
        with eng.Fori(start + 1, n) as i:
            body(i)

    def load8(eng, regs, table, at):
        eng.load(regs, table[0:1, ds(at, 8)])
        return [eng.snap(r, min_val=0, max_val=BLOCKS - 1) for r in regs]

    def dram(name, shape, dt):
        return nc.dram_tensor(name, shape, dt, kind="Internal").ap()

    k_tab = dram("k_tab", (BLOCKS * P, D), f32)
    v_tab = dram("v_tab", (RL * P, D), f32)
    seg_d = dram("seg_d", (TROWS * P,), bf16)
    loc_d = dram("loc_d", (TROWS * P,), bf16)
    blk_d = dram("blk_d", (TROWS,), i32)

    with ctx:
        R = sb("R", [P, BLOCKS * W])
        E = sb("E", [P, (RL + 1) * P])
        wq = sb("wq", [P, KC, D])
        wv = sb("wv", [P, KC, D])
        w1 = sb("w1", [P, KC, DFF])
        w2 = sb("w2", [P, FC, D])
        ring = sb("ring", [P, RING, D])
        prod = sb("prod", [P, 4, D])
        oh = sb("oh", [P, 2, 8, P])
        loc = sb("loc", [P, 2, 8 * P], bf16)
        xt = sb("xt", [P, 2, KC, P])
        vout = sb("vout", [P, D])
        src_t = sb("src_t", [P, TROWS], i32)
        loc_t = sb("loc_t", [P, TROWS], bf16)
        inv_t = sb("inv_t", [P, TROWS], bf16)
        blk1 = sb("blk1", [1, STEPS], i32)
        blk3 = sb("blk3", [1, STEPS], i32)
        idx = sb("idx", [P, 2, 8], i32)
        ident = sb("ident", [P, P])
        iota_row = sb("iota_row", [P, P], bf16)
        iota_col = sb("iota_col", [P, 1])
        one = sb("one", [1, 1])
        b1_col = sb("b1_col", [P, FC])
        g1_col = sb("g1_col", [P, KC])
        o1_col = sb("o1_col", [P, KC])
        eps = sb("eps", [P, 1])
        est = sb("est", [P, HEADS, UN])
        junk = sb("junk", [P, DK])

        q_blk = R[:, :].rearrange("p (b w) -> p b w", w=W)
        wk = ring[:, 0:KC, :]
        e_all = E[:, 0:HEADS * STEPS].rearrange("p (h s) -> p h s", h=HEADS)

        s_wk = sem("wk_in")
        s_w, s_w2, s_pc = sem("wq_in"), sem("weights_in"), sem("pool_constants")
        s_x = [sem(f"xt_in{i}") for i in range(2)]
        s_qps, s_kps = sem("q_product_done"), sem("k_product_done")
        s_qout, s_kout = sem("q_copied"), sem("k_copied")
        s_kst = [sem(f"k_stored{i}") for i in range(2)]
        s_tin, s_const, s_tab = sem("table_inputs_in"), sem("constants_ready"), sem("tables_done")
        s_tidx, s_tg = sem("tile_index_ready"), sem("edge_rows_in")
        s_tT, s_tTc = sem("table_transposed"), sem("table_copied")
        s_rows, s_tst, s_tld = sem("table_rows_ready"), sem("table_rows_stored"), sem("block_rows_in")
        s_dc = sem("vector_chain")
        chain = [0]

        def link(dve, ins):
            chain[0] += 1
            ins.then_inc(s_dc, 1)
            dve.wait_ge(s_dc, chain[0])

        TB = 34 * W
        N3 = GROUPS * P

        def tmp(n, cols=N3):
            return R[:, TB + n * N3:TB + n * N3 + cols]

        last_i, lastf, key = (E[:, i * TILES:(i + 1) * TILES] for i in range(3))
        rows_i = tmp(0, 3 * N3).bitcast(i32).rearrange("p (g w) -> p g w", g=GROUPS)
        dstf = tmp(3).rearrange("p (g w) -> p g w", g=GROUPS)
        prevf = tmp(4).rearrange("p (g w) -> p g w", g=GROUPS)
        srcf = tmp(5).rearrange("p (g w) -> p g w", g=GROUPS)
        valid = tmp(6).rearrange("p (g w) -> p g w", g=GROUPS)
        packed = tmp(7, N3).bitcast(bf16).rearrange("p (k g w) -> p k g w", k=2, g=GROUPS)
        small = E[:, 3 * TILES:3 * TILES + 64]
        scol, tstep, bstep, base = (small[:, i * 8:i * 8 + GROUPS] for i in range(4))
        scol_i, tstep_i, bstep_i = (small[:, 32 + i * 8:32 + i * 8 + GROUPS].bitcast(i32) for i in range(3))
        iota_t = E[:, 4 * TILES:5 * TILES]
        iota_ti = E[:, 5 * TILES:6 * TILES].bitcast(i32)
        iota_ri = E[:, 6 * TILES:6 * TILES + P].bitcast(i32)
        iota_ci = E[:, 6 * TILES + P:6 * TILES + P + 1].bitcast(i32)


        kout = prod[:, 0:2, :]
        x_tile = lambda t: a["xt"][ds(t, 1)].rearrange("a p k n -> p (a k) n")


        kout = prod[:, 0:2, :]
        x_tile = lambda t: a["xt"][ds(t, 1)].rearrange("a p k n -> p (a k) n")

        with nc.psum_tensor("ps_q", [P, 2, D], f32) as ps_q, \
                nc.psum_tensor("ps_k", [P, 2, D], f32) as ps_k, \
                nc.psum_tensor("ps_t", [P, 2, D], f32) as ps_t, nc.Block(no_gpsimd_drain=True) as block:

            @block.sync
            def _(sp):
                sp.dma_start(last_i.bitcast(i32), a["tile_last"][0:1, :].to_broadcast([P, TILES])).then_inc(s_tin, 16)
                sp.dma_start(wq[:], a["wq"]).then_inc(s_w, 16)

                def load(t, slot):
                    wait(sp, s_kps, t - 1)
                    sp.dma_start(xt[:, slot], x_tile(t)).then_inc(s_x[slot], 16)

                def store(t, slot):
                    wait(sp, s_kout, t + 1)
                    sp.dma_start(k_tab[ds(t * P, P), :], kout[:, slot]).then_inc(s_kst[slot], 16)

                def pair(i):
                    for slot in range(2):
                        t = 2 * i + slot
                        load(t, slot)
                        if isinstance(t, int) and t == 0:
                            sp.dma_start(wk, a["wk"]).then_inc(s_wk, 16)
                        if isinstance(t, int) and t == 1:
                            sp.dma_start(wv[:], a["wv"]).then_inc(s_w2, 16)
                            sp.dma_start(w1[:], a["w1"]).then_inc(s_w2, 16)
                            sp.dma_start(w2[:], a["w2"]).then_inc(s_w2, 16)
                        if not (isinstance(t, int) and t == 0):
                            store(t - 1, 1 - slot)

                pair(0)
                with sp.Fori(1, 8) as i:
                    pair(i)
                sp.wait_ge(s_rows, 1)
                for n, t in enumerate((seg_d, loc_d)):
                    sp.dma_start(t.rearrange("(g p w) -> p g w", p=P, w=P), packed[:, n]).then_inc(s_tst, 16)
                with nc.allow_non_contiguous_dma(reason="896 block numbers, once"):
                    sp.dma_start(blk_d.rearrange("(g p) -> p g", p=P), bstep_i).then_inc(s_tst, 16)
                    sp.wait_ge(s_tst, 48)
                    sp.dma_start(blk1[:], blk_d[0:STEPS].rearrange("(a s) -> a s", a=1)).then_inc(s_tld, 16)
                    sp.dma_start(blk3[:].rearrange("a (c j) -> a c j", j=RUNS),
                                 blk_d[0:STEPS].rearrange("(a j c) -> a c j", a=1, j=RUNS)).then_inc(s_tld, 16)
                with sp.Fori(8, BLOCKS // 2) as i:
                    pair(i)
                load(BLOCKS - 1, 0)
                store(BLOCKS - 2, 1)
                store(BLOCKS - 1, 0)
                sp.wait_ge(s_w2, 48)
                sp.wait_ge(s_tld, 32)
                sp.wait_ge(s_kst[0], 16 * (BLOCKS // 2 + 1))
                sp.wait_ge(s_kst[1], 16 * (BLOCKS // 2))

            @block.tensor
            def _(pe):
                pe.wait_ge(s_w, 16)

                def tile(i, slot):
                    t = 2 * i + slot
                    wait(pe, s_x[slot], 16 * (i + 1))
                    wait(pe, s_qout, t - 1)
                    wait(pe, s_kout, t - 1)
                    for ps, w, done in ((ps_q, wq, s_qps), (ps_k, wk, s_kps)):
                        if isinstance(t, int) and t == 0 and w is wk:
                            pe.wait_ge(s_wk, 16)
                        for c in range(KC):
                            last = nc.tensor.matmul(ps[:, slot, :], xt[:, slot, c, :], w[:, c, :],
                                                    start=(c == 0), stop=(c == KC - 1))
                        last.then_inc(done, 1)

                def pair(i):
                    tile(i, 0)
                    tile(i, 1)

                pair(0)
                with pe.Fori(1, 8) as i:
                    pair(i)
                pe.wait_ge(s_const, 1)
                pe.wait_ge(s_rows, 1)
                for g in range(GROUPS):
                    for n, what in ((0, srcf), (1, dstf)):
                        wait(pe, s_tTc, 2 * g + n - 1)
                        nc.tensor.transpose(ps_t[:, n, 0:P], what[:, g, :], ident[:]).then_inc(s_tT, 1)
                with pe.Fori(8, BLOCKS // 2) as i:
                    pair(i)
                tile(BLOCKS // 2, 0)

            @block.scalar
            def _(act):
                def tile(i, slot):
                    t = 2 * i + slot
                    wait(act, s_qps, t + 1)
                    nc.scalar.activation(q_blk[:, ds(t, 1), 0:D].rearrange("p a w -> p (a w)"),
                                         ps_q[:, slot, :], ACT.Copy).then_inc(s_qout, 1)
                    wait(act, s_kps, t + 1)
                    wait(act, s_kst[slot], 16 * i)
                    nc.scalar.activation(kout[:, slot, :], ps_k[:, slot, :], ACT.Copy).then_inc(s_kout, 1)

                def pair(i):
                    tile(i, 0)
                    tile(i, 1)

                pair(0)
                with act.Fori(1, 12) as i:
                    pair(i)
                act.wait_ge(s_tTc, 2 * GROUPS)
                act.wait_ge(s_tst, 48)
                with act.Fori(12, BLOCKS // 2) as i:
                    pair(i)
                tile(BLOCKS // 2, 0)

            @block.gpsimd
            def _(pool):
                nc.gpsimd.memset(ident[:], 0.0).then_inc(s_pc, 1)
                nc.gpsimd.iota(iota_ti, [[1, TILES]], base=0, channel_multiplier=0).then_inc(s_pc, 1)
                nc.gpsimd.iota(scol_i, [[P, GROUPS]], base=0, channel_multiplier=1).then_inc(s_pc, 1)
                nc.gpsimd.iota(iota_ri, [[1, P]], base=0, channel_multiplier=0).then_inc(s_pc, 1)
                nc.gpsimd.iota(iota_ci, [[0, 1]], base=0, channel_multiplier=1).then_inc(s_pc, 1)
                nc.gpsimd.memset(one[:], 1.0).then_inc(s_pc, 1)
                nc.gpsimd.memset(ring[:, KC:RING, :], 0.0)
                nc.gpsimd.memset(eps[:], EPS)
                pool.wait_ge(s_pc, 1)
                nc.gpsimd.affine_select(out=ident[:], in_=ident[:], compare_op=ALU.not_equal, fill=1.0,
                                        base=0, pattern=[[-1, P]], channel_multiplier=1).then_inc(s_const, 1)
                pool.wait_ge(s_tidx, 1)
                for g in range(GROUPS):
                    pool.indirect_dma_start(out=rows_i[:, g, :], out_offset=None, in_=a["edges"],
                                            in_offset=bass.IndirectOffsetOnAxis(ap=tstep_i[:, g:g + 1], axis=0),
                                            bounds_check=TILES - 1, oob_is_err=False).then_inc(s_tg, 16)
                pool.wait_ge(s_tg, 16 * GROUPS)

            @block.vector
            def _(dve):
                v = nc.vector
                dve.wait_ge(s_tin, 16)
                dve.wait_ge(s_pc, 6)
                v.tensor_copy(iota_row[:], iota_ri)
                v.tensor_copy(iota_col[:], iota_ci)
                v.tensor_copy(scol, scol_i)
                v.tensor_copy(iota_t, iota_ti)
                link(dve, v.tensor_single_scalar(last_i.bitcast(i32), last_i.bitcast(i32), 7, ALU.arith_shift_right))
                link(dve, v.tensor_copy(lastf, last_i.bitcast(i32)))
                link(dve, v.tensor_tensor(key, lastf, iota_t, ALU.add))
                for g in range(GROUPS):
                    link(dve, v.tensor_scalar(lastf, key, scol[:, g:g + 1], 0.0, ALU.is_lt, ALU.add,
                                              accum_out=tstep[:, g:g + 1]))
                link(dve, v.tensor_scalar_min(tstep, tstep, float(TILES - 1)))
                v.tensor_copy(tstep_i, tstep).then_inc(s_tidx, 1)
                link(dve, v.tensor_tensor(bstep, scol, tstep, ALU.subtract))
                link(dve, v.tensor_copy(bstep_i, bstep))
                link(dve, v.tensor_scalar_mul(base, bstep, float(P)))
                dve.wait_ge(s_tg, 16 * GROUPS)
                v.tensor_copy(srcf, rows_i[:, :, 0:P])
                v.tensor_copy(prevf, rows_i[:, :, 2 * P:3 * P])
                link(dve, v.tensor_copy(dstf, rows_i[:, :, P:2 * P]))
                link(dve, v.tensor_tensor(prevf, dstf, prevf, ALU.not_equal))
                for g in range(GROUPS):
                    ins = v.tensor_scalar(dstf[:, g, :], dstf[:, g, :], base[:, g:g + 1], None, ALU.subtract)
                link(dve, ins)
                link(dve, v.tensor_scalar(valid, dstf, 0.0, None, ALU.is_ge))
                link(dve, v.scalar_tensor_tensor(valid, dstf, float(P - 1), valid, ALU.is_le, ALU.mult))
                v.scalar_tensor_tensor(packed[:, 0], prevf, -BIG, valid, ALU.mult, ALU.mult)
                link(dve, v.scalar_tensor_tensor(dstf, dstf, -255.0, valid, ALU.add, ALU.mult))
                link(dve, v.tensor_scalar_add(dstf, dstf, 255.0))
                link(dve, v.tensor_copy(packed[:, 1], dstf))
                link(dve, v.tensor_scalar(valid, valid, -float(SKIP), float(SKIP), ALU.mult, ALU.add))
                v.tensor_tensor(srcf, srcf, valid, ALU.add).then_inc(s_rows, 1)
                for g in range(GROUPS):
                    for n, to in ((0, src_t), (1, loc_t)):
                        dve.wait_ge(s_tT, 2 * g + n + 1)
                        v.tensor_copy(to[:, g * P:(g + 1) * P], ps_t[:, n, 0:P]).then_inc(s_tTc, 1)
                dve.wait_ge(s_tTc, 2 * GROUPS)
                link(dve, v.tensor_scalar(inv_t[:], loc_t[:], float(P), -BIG, ALU.is_ge, ALU.mult))

        s_idx = sem("index_columns_ready")
        s_k = [sem(f"k_rows_in{i}") for i in range(RING)]
        s_loc = [sem(f"loc_in{i}") for i in range(2)]
        s_oh, s_qx, s_mul, s_sum = sem("onehot_ready"), sem("q_expanded"), sem("product_ready"), sem("scalar_heads_summed")
        s_red, s_xv, s_vps, s_vout, s_vst = (sem(n) for n in ("vector_heads_summed", "xt_for_v_in", "v_product_done", "v_copied", "v_stored"))
        s_mc = sem("scores_moved")

        def load_loc(sp, n, half):
            sp.dma_start(loc[:, half], loc_d[ds(n * 8 * P, 8 * P)].rearrange("(a w) -> a w", a=1)
                         .to_broadcast([P, 8 * P])).then_inc(s_loc[half], 16)

        with nc.psum_tensor("ps_qx", [P, 4, D], f32) as ps_qx, \
                nc.psum_tensor("ps_v", [P, D], f32) as ps_v, nc.Block(no_gpsimd_drain=True) as block:

            @block.sync
            def _(sp):
                load_loc(sp, 0, 0)
                load_loc(sp, 1, 1)
                sp.dma_start(xt[:, 0], x_tile(0)).then_inc(s_xv, 16)

                def body(i):
                    for half in range(2):
                        n = 2 * i + 2 + half
                        wait(sp, s_oh, n - 1)
                        load_loc(sp, n, half)
                    wait(sp, s_vout, i + 1)
                    sp.dma_start(v_tab[ds(i * P, P), :], vout[:]).then_inc(s_vst, 16)
                    wait(sp, s_vst, 16 * (i + 1))
                    sp.dma_start(xt[:, 0], x_tile(i + 1)).then_inc(s_xv, 16)

                repeat(sp, RL, body)
                for half in range(2):
                    sp.wait_ge(s_loc[half], 16 * (RL + 1))
                sp.wait_ge(s_xv, 16 * (RL + 1))

            @block.gpsimd
            def _(pool):
                bound = pool.to_reg(BLOCKS * P - 1)

                def body(i):
                    for half in range(2):
                        s = UN * i + 8 * half
                        wait(pool, s_mul, s - 7)
                        nc.gpsimd.tensor_copy(idx[:, half, :], src_t[:, ds(s, 8)]).then_inc(s_idx, 1)
                        wait(pool, s_idx, 2 * i + half + 1)
                        for u in range(8):
                            wait(pool, s_mul, s + u - 7)
                            pool.indirect_dma_start(out=ring[:, u, :], out_offset=None, in_=k_tab,
                                                    in_offset=bass.IndirectOffsetOnAxis(ap=idx[:, half, u:u + 1], axis=0),
                                                    bounds_check=bound, oob_is_err=False).then_inc(s_k[u], 16)

                repeat(pool, RL, body)

            @block.tensor
            def _(pe):
                regs = [pe.alloc_register(f"pe_blk{u}") for u in range(8)]

                def body(i):
                    for half in range(2):
                        blk = load8(pe, regs, blk1, UN * i + 8 * half)
                        wait(pe, s_oh, 2 * i + half + 1)
                        for u in range(8):
                            s = UN * i + 8 * half + u
                            wait(pe, s_mul, s - 3)
                            nc.tensor.matmul(ps_qx[:, u % 4, :], oh[:, half, u, :],
                                             q_blk[:, ds(blk[u], 1), 0:D].rearrange("p a w -> p (a w)"),
                                             start=True, stop=True).then_inc(s_qx, 1)
                            if half and u % 2:
                                c = u // 2
                                if c == 0:
                                    wait(pe, s_xv, 16 * (i + 1))
                                last = nc.tensor.matmul(ps_v[:], xt[:, 0, c, :], wv[:, c, :],
                                                        start=(c == 0), stop=(c == KC - 1))
                                if c == KC - 1:
                                    last.then_inc(s_vps, 1)

                repeat(pe, RL, body)

            @block.vector
            def _(dve):
                def build(n, half):
                    wait(dve, s_loc[half], 16 * ((n - half) // 2 + 1) if isinstance(n, int) else 8 * (n - half) + 16)
                    wait(dve, s_qx, 8 * (n - 1))
                    nc.vector.tensor_scalar(oh[:, half].rearrange("p u w -> p (u w)"), loc[:, half],
                                            iota_col[:, 0:1], None, ALU.is_equal).then_inc(s_oh, 1)

                build(0, 0)

                def body(i):
                    for u in range(UN):
                        s = UN * i + u
                        if u == 4:
                            build(2 * i + 1, 1)
                        if u == 12:
                            build(2 * i + 2, 0)
                        wait(dve, s_qx, s + 1)
                        wait(dve, s_k[u % 8], 32 * i + 16 * (u // 8 + 1))
                        wait(dve, s_sum, s - 3)
                        nc.vector.tensor_tensor(prod[:, u % 4, :], ps_qx[:, u % 4, :], ring[:, u % 8, :],
                                                ALU.mult).then_inc(s_mul, 1)
                        if not (isinstance(s, int) and s == 0):
                            sums(s - 1, (u - 1) % UN)
                        if u == 10:
                            move(2 * i, 0)
                        if u == 2 and not isinstance(i, int):
                            move(2 * i - 1, 1)

                def sums(s, u):
                    wait(dve, s_mul, s + 1)
                    nc.vector.tensor_reduce(est[:, 0:SUM_HEADS, u], prod[:, u % 4, 0:SUM_HEADS * DK]
                                            .rearrange("p (h d) -> p h d", h=SUM_HEADS), AX.X, ALU.add).then_inc(s_red, 1)

                def move(n, half):
                    wait(dve, s_red, 8 * n + 8)
                    wait(dve, s_sum, 8 * n + 8)
                    nc.vector.tensor_tensor(e_all[:, :, ds(8 * n, 8)], est[:, :, 8 * half:8 * half + 8],
                                            inv_t[:, ds(8 * n, 8)].unsqueeze(1).to_broadcast([P, HEADS, 8]),
                                            ALU.add).then_inc(s_mc, 1)

                repeat(dve, RL, body)
                sums(STEPS - 1, UN - 1)
                move(2 * RL - 1, 1)

            @block.scalar
            def _(act):
                def body(i):
                    for u in range(UN):
                        s = UN * i + u
                        wait(act, s_mul, s + 1)
                        wait(act, s_mc, 2 * i - 1 + u // 8)
                        for h in range(SUM_HEADS, HEADS):
                            part = prod[:, u % 4, h * DK:(h + 1) * DK]
                            ins = nc.scalar.activation(part, part, ACT.Copy,
                                                       accum_out=est[:, h, u:u + 1])
                        ins.then_inc(s_sum, 1)
                    wait(act, s_vps, i + 1)
                    nc.scalar.activation(vout[:], ps_v[:], ACT.Copy).then_inc(s_vout, 1)

                repeat(act, RL, body)

        s_mi = sem("masks_in")
        s_sc, s_eT, s_eM = sem("scores_staged"), sem("scores_transposed"), sem("scores_masked")
        s_col, s_colT, s_row, s_rowT = sem("ends_ready"), sem("ends_transposed"), sem("carries_ready"), sem("carries_transposed")
        s_wc, s_bp = sem("columns_in"), sem("folded_bias_product")
        s_max, s_any = sem("maxima_done"), sem("starts_summed")
        s_dead, s_zero, s_wo = sem("maxima_used"), sem("sums_cleared"), sem("late_weights_in")

        sc_t = R[:, 0:RE]
        mx_t = R[:, RE:2 * RE]
        seg_t = R[:, 2 * RE:2 * RE + RE // 2 + 2].bitcast(bf16)
        work_end = 2 * RE + RE // 2 + 2
        stage = prod[:, 0:2, :]
        cols = est[:, 0, 0:8]
        rows = oh[0:1, 0, :, :]
        e_runs = e_all.rearrange("p h (j c) -> p c h j", c=RL)

        def units(eng, unit):
            def pair(i):
                unit(2 * i, 0)
                unit(2 * i + 1, 1)
            repeat(eng, RL // 8, pair)
            unit(RL // 4 - 1, 0)

        gains = [wv[:, c, :] for c in range(4)] + [vout[:]]

        cut = 4352
        z1, z2 = 5400, 11600
        sc_any = E[:, 0:z2 - z1]

        s_v = [sem(f"v_rows_in{i}") for i in range(RING)]
        s_idx3 = sem("v_index_columns_ready")
        src_c = src_t[:, 0:STEPS].rearrange("p (j c) -> p c j", c=RL)

        def gather8(pool, i, q, bound):
            par, half = divmod(q, 2)
            s = 2 * UN * i + 8 * q
            wait(pool, s_wd, s - 7)
            wait(pool, s_wa, s - 7)
            nc.gpsimd.tensor_copy(idx[:, half, :], src_c[:, ds(2 * i + par, 1), 8 * half:8 * half + 8]
                                  .rearrange("p c j -> p (c j)")).then_inc(s_idx3, 1)
            wait(pool, s_idx3, 4 * i + q + 1)
            for u in range(8):
                wait(pool, s_wd, s + u - 7)
                wait(pool, s_wa, s + u - 7)
                pool.indirect_dma_start(out=ring[:, u, :], out_offset=None, in_=v_tab,
                                        in_offset=bass.IndirectOffsetOnAxis(ap=idx[:, half, u:u + 1], axis=0),
                                        bounds_check=bound, oob_is_err=False).then_inc(s_v[u], 16)

        s_wd, s_wa = sem("vector_heads_weighted"), sem("scalar_heads_weighted")

        with nc.psum_tensor("ps_e", [P, 2, D], f32) as ps_e, \
                nc.psum_tensor("ps_c", [P, 2, D], f32) as ps_c, \
                nc.psum_tensor("ps_b", [P, D], f32) as ps_b, nc.Block(no_gpsimd_drain=True) as block:

            @block.sync
            def _(sp):
                for h in range(HEADS):
                    at = slice(h * RUNS, (h + 1) * RUNS)
                    sp.dma_start(seg_t[at, 0:RE], seg_d[0:RUNS * RE].rearrange("(j w) -> j w", j=RUNS)).then_inc(s_mi, 16)
                    with nc.allow_non_contiguous_dma(reason="the first slot of the next run, 16 values"):
                        sp.dma_start(seg_t[at, RE:RE + 1], seg_d[RE:(RUNS + 1) * RE].rearrange("(j w) -> j w", j=RUNS)[:, 0:1]).then_inc(s_mi, 16)
                sp.dma_start(wq[:], a["wo"]).then_inc(s_wo, 16)
                for name, to in zip(("ln1_g", "ln1_b", "ln2_g", "ln2_b", "b2"), gains):
                    sp.dma_start(to, a[name].to_broadcast([P, D])).then_inc(s_wo, 16)
                for name, to in (("b1", b1_col), ("g1_col", g1_col), ("o1_col", o1_col)):
                    sp.dma_start(to[:], a[name]).then_inc(s_wc, 16)
                sp.wait_ge(s_wc, 48)
                sp.wait_ge(s_mi, 16 * 2 * HEADS)
                sp.wait_ge(s_wo, 16 * 6)

            @block.scalar
            def _(act):
                def unit(n, slot):
                    wait(act, s_eT, n - 1)
                    nc.scalar.activation(stage[:, slot, :].rearrange("p (c h j) -> p c h j", c=4, h=HEADS),
                                         e_runs[:, ds(4 * n, 4), :, :], ACT.Copy).then_inc(s_sc, 1)

                units(act, unit)
                act.wait_ge(s_mi, 16 * 2 * HEADS)
                for way in range(2):
                    nc.scalar.activation(mx_t, seg_t[:, way:RE + way], ACT.Copy, scale=2.0 ** -20,
                                         accum_out=cols[:, 2 * way + 1:2 * way + 2]).then_inc(s_any, 1)
                    act.wait_ge(s_any, way + 1)
                act.wait_ge(s_bp, 1)
                for j in range(FC):
                    nc.scalar.activation(b1_col[:, j:j + 1], ps_b[:, j:j + 1], ACT.Identity, bias=b1_col[:, j:j + 1])
                for c in range(KC):
                    nc.scalar.activation(w1[:, c, :], w1[:, c, :], ACT.Copy, scale=g1_col[:, c:c + 1])
                act.wait_ge(s_dead, 2)
                nc.scalar.activation(R[:, z1:z2], sc_any, ACT.Copy, scale=0.0).then_inc(s_zero, 1)

            @block.tensor
            def _(pe):
                def unit(n, slot):
                    wait(pe, s_sc, n + 1)
                    wait(pe, s_eM, n - 1)
                    for c in range(4):
                        ins = nc.tensor.transpose(ps_e[:, slot, c * P:(c + 1) * P],
                                                  stage[:, slot, c * P:(c + 1) * P], ident[:])
                    ins.then_inc(s_eT, 1)

                units(pe, unit)
                pe.wait_ge(s_wc, 48)
                for j in range(FC):
                    for c in range(KC):
                        ins = nc.tensor.matmul(ps_b[:, j:j + 1], w1[:, c, j * P:(j + 1) * P], o1_col[:, c:c + 1],
                                               start=(c == 0), stop=(c == KC - 1))
                ins.then_inc(s_bp, 1)
                for way in range(2):
                    pe.wait_ge(s_col, way + 1)
                    for n in range(2):
                        ins = nc.tensor.transpose(ps_c[0:1, 0, n * P:(n + 1) * P], cols[:, 2 * way + n:2 * way + n + 1], ident[:])
                    ins.then_inc(s_colT, 1)
                    pe.wait_ge(s_row, way + 1)
                    nc.tensor.matmul(ps_c[:, 1, 0:1], rows[0:1, 4 * way + 3, :], one[0:1, 0:1],
                                     start=True, stop=True).then_inc(s_rowT, 1)

            @block.gpsimd
            def _(pool):
                gather8(pool, 0, 0, BLOCKS * P - 1)
                nc.gpsimd.memset(R[:, work_end:BLOCKS * W], 0.0).then_inc(s_zero, 1)
                pool.wait_ge(s_wo, 16 * 6)
                nc.gpsimd.tensor_tensor(gains[1], gains[1], gains[4], ALU.add)
                pool.wait_ge(s_max, 1)
                nc.gpsimd.tensor_tensor(E[:, cut:RE], sc_t[:, cut:RE], mx_t[:, cut:RE], ALU.subtract).then_inc(s_dead, 1)
                pool.wait_ge(s_dead, 2)
                nc.gpsimd.memset(R[:, z2:work_end], 0.0).then_inc(s_zero, 1)

            @block.vector
            def _(dve):
                v = nc.vector
                def unit(n, slot):
                    wait(dve, s_eT, n + 1)
                    v.tensor_copy(sc_t[:, ds(4 * P * n, 4 * P)], ps_e[:, slot, :]).then_inc(s_eM, 1)

                units(dve, unit)
                dve.wait_ge(s_eM, RL // 4)
                dve.wait_ge(s_mi, 16 * 2 * HEADS)

                for way, (reset, data) in enumerate(((seg_t[:, 0:RE], sc_t),
                                                         (seg_t[:, RE:0:-1], mx_t[:, ::-1]))):
                    end = RE - 1 if way == 0 else 0
                    trial = E[:, 0:RE] if way == 0 else E[:, 0:RE][:, ::-1]
                    link(dve, v.tensor_tensor_scan(trial, reset, data, -BIG, ALU.add, ALU.max))
                    v.tensor_copy(cols[:, 2 * way:2 * way + 1], E[:, end:end + 1])
                    dve.wait_ge(s_any, 2)
                    v.tensor_scalar(cols[:, 2 * way + 1:2 * way + 2], cols[:, 2 * way + 1:2 * way + 2],
                                    0.0, -BIG, ALU.is_lt, ALU.mult).then_inc(s_col, 1)
                    dve.wait_ge(s_colT, way + 1)
                    got, res, inc, carry = (rows[0:1, 4 * way + n, :] for n in range(4))
                    heads = lambda r: r.rearrange("a (h j) -> a h j", h=HEADS)
                    v.tensor_copy(got, ps_c[0:1, 0, 0:P])
                    link(dve, v.tensor_copy(res, ps_c[0:1, 0, P:2 * P]))
                    first = 0 if way == 0 else RUNS - 1
                    v.memset(carry, -BIG)
                    link(dve, v.memset(heads(res)[:, :, first:first + 1], -BIG))
                    if way == 0:
                        link(dve, v.tensor_tensor_scan(inc, res, got, -BIG, ALU.add, ALU.max))
                        v.tensor_copy(heads(carry)[:, :, 1:RUNS], heads(inc)[:, :, 0:RUNS - 1]).then_inc(s_row, 1)
                    else:
                        link(dve, v.tensor_tensor_scan(inc[:, ::-1], res[:, ::-1], got[:, ::-1], -BIG, ALU.add, ALU.max))
                        v.tensor_copy(heads(carry)[:, :, 0:RUNS - 1], heads(inc)[:, :, 1:RUNS]).then_inc(s_row, 1)
                    dve.wait_ge(s_rowT, way + 1)
                    link(dve, v.tensor_copy(cols[:, 4 + way:5 + way], ps_c[:, 1, 0:1]))
                    link(dve, v.tensor_tensor_scan(mx_t if way == 0 else mx_t[:, ::-1], reset, data,
                                                   cols[:, 4 + way:5 + way], ALU.add, ALU.max))
                v.memset(E[:, RE:RE + P], 0.0).then_inc(s_max, 1)
                v.tensor_tensor(E[:, 0:cut], sc_t[:, 0:cut], mx_t[:, 0:cut], ALU.subtract).then_inc(s_dead, 1)
                dve.wait_ge(s_dead, 2)
                v.memset(R[:, 0:z1], 0.0).then_inc(s_zero, 1)

        s_loc3, s_oh3 = sem("loc_columns_ready"), sem("v_onehot_ready")
        s_exp, s_exT, s_exc = sem("weights_ready"), sem("weights_transposed"), sem("weights_copied")
        s_pv, s_acc = sem("step_summed"), sem("step_added")
        loc_c = loc_t[:, 0:STEPS].rearrange("p (j c) -> p c j", c=RL)
        oht = oh[:, 0, 0:4, :]
        exs = oh[:, 0, 4:6, :]
        exl = oh[:, 0, 6:8, :]
        locr = est[:, 0:2, :]

        with nc.psum_tensor("ps_a", [P, 2, 2 * D], f32) as ps_a, \
                nc.psum_tensor("ps_ex", [P, 2, D], f32) as ps_ex, nc.Block(no_gpsimd_drain=True) as block:

            @block.gpsimd
            def _(pool):
                bound = pool.to_reg(BLOCKS * P - 1)

                def body(i):
                    for q in range(4):
                        if not (isinstance(i, int) and q == 0):
                            gather8(pool, i, q, bound)

                repeat(pool, RL // 2, body)

            @block.scalar
            def _(act):
                def weights(c, slot):
                    wait(act, s_exT, c - 1)
                    nc.scalar.activation(exs[:, slot, :], E[:, ds(c * P, P)], ACT.Exp, scale=DK ** -0.5).then_inc(s_exp, 1)

                def copies(c, slot):
                    wait(act, s_exT, c + 1)
                    wait(act, s_pv, UN * (c - 1))
                    nc.scalar.activation(exl[:, slot, :], ps_ex[:, slot, 0:P], ACT.Copy).then_inc(s_exc, 1)

                weights(0, 0)
                copies(0, 0)

                def body(i):
                    for par in range(2):
                        c = 2 * i + par
                        for j in range(UN):
                            s = UN * c + j
                            if j == 6:
                                weights(c + 1, 1 - par)
                            if j == 12:
                                copies(c + 1, 1 - par)
                            if j == 0:
                                wait(act, s_exc, c + 1)
                            wait(act, s_v[j % 8], 32 * c + 16 * (j // 8 + 1))
                            wait(act, s_pv, s - 3)
                            for h in range(MUL_HEADS, HEADS):
                                ins = nc.scalar.activation(prod[:, j % 4, h * DK:(h + 1) * DK],
                                                           ring[:, j % 8, h * DK:(h + 1) * DK], ACT.Copy,
                                                           scale=exl[:, par, h * RUNS + j:h * RUNS + j + 1])
                            ins.then_inc(s_wa, 1)

                repeat(act, RL // 2, body)

            @block.tensor
            def _(pe):
                def turn(c, slot):
                    wait(pe, s_exp, c + 1)
                    wait(pe, s_wd, UN * (c - 1))
                    wait(pe, s_exc, c - 1)
                    nc.tensor.transpose(ps_ex[:, slot, 0:P], exs[:, slot, :], ident[:]).then_inc(s_exT, 1)

                turn(0, 0)

                def body(i):
                    for par in range(2):
                        c = 2 * i + par
                        for j in range(UN):
                            s = UN * c + j
                            if j == 10:
                                turn(c + 1, 1 - par)
                            if j == 0:
                                wait(pe, s_exc, c + 1)
                            wait(pe, s_oh3, s + 1)
                            wait(pe, s_wd, s + 1)
                            wait(pe, s_wa, s + 1)
                            wait(pe, s_acc, s - 1)
                            nc.tensor.matmul(ps_a[:, j % 2, 0:D], oht[:, j % 4, :], prod[:, j % 4, :],
                                             start=True, stop=True)
                            nc.tensor.matmul(ps_a[:, j % 2, D:W], oht[:, j % 4, :],
                                             exl[:, par, :].rearrange("p (h j) -> p h j", h=HEADS)[:, :, j],
                                             start=True, stop=True).then_inc(s_pv, 1)

                repeat(pe, RL // 2, body)

            @block.vector
            def _(dve):
                v = nc.vector
                regs = [dve.alloc_register(f"dve_blk{u}") for u in range(8)]
                dve.wait_ge(s_zero, 4)
                late = [dve.alloc_register(f"dve_late{u}") for u in range(4)]

                def add(s, n, blk):
                    to = q_blk[:, ds(blk, 1), :].rearrange("p a w -> p (a w)")
                    wait(dve, s_pv, s + 1)
                    wait(dve, s_acc, s)
                    v.tensor_tensor(to, to, ps_a[:, n % 2, 0:W], ALU.add).then_inc(s_acc, 1)

                def last_two(s):
                    dve.load(late, blk3[0:1, ds(s - 4, 4)])
                    return [dve.snap(r, min_val=0, max_val=BLOCKS - 1) for r in late[2:]]

                def body(i):
                    before = None if isinstance(i, int) else last_two(2 * UN * i)
                    for par in range(2):
                        c = 2 * i + par
                        wait(dve, s_oh3, UN * (c - 1))
                        v.tensor_copy(locr[:, par, :], loc_c[:, ds(c, 1), :].rearrange("p c j -> p (c j)")).then_inc(s_loc3, 1)
                        wait(dve, s_loc3, c + 1)
                        for j in range(UN):
                            s = UN * c + j
                            wait(dve, s_pv, s - 3)
                            v.tensor_scalar(oht[:, j % 4, :], iota_row[:], locr[:, par, j:j + 1], None,
                                            ALU.is_equal).then_inc(s_oh3, 1)
                            wait(dve, s_exc, c + 1)
                            wait(dve, s_v[j % 8], 32 * c + 16 * (j // 8 + 1))
                            n = MUL_HEADS
                            v.tensor_tensor(prod[:, j % 4, 0:n * DK].rearrange("p (h d) -> p h d", h=n),
                                            ring[:, j % 8, 0:n * DK].rearrange("p (h d) -> p h d", h=n),
                                            ps_ex[:, par, 0:P].rearrange("p (h j) -> p h j", h=HEADS)[:, 0:n, j:j + 1]
                                            .to_broadcast([P, n, DK]), ALU.mult).then_inc(s_wd, 1)
                            n = UN * par + j - 2
                            if n >= 0:
                                if n % 8 == 0:
                                    blk = load8(dve, regs, blk3, 2 * UN * i + n)
                                add(s - 2, n, blk[n % 8])
                            elif before:
                                add(s - 2, n % 2, before[n + 2])

                repeat(dve, RL // 2, body)
                for n, blk in enumerate(last_two(STEPS)):
                    add(STEPS - 2 + n, n, blk)

        s_xa = [sem(f"x_for_residual1_in{i}") for i in range(2)]
        s_xb = [sem(f"x_for_residual2_in{i}") for i in range(2)]
        s_st = [sem(f"out_stored{i}") for i in range(2)]
        names = ("rz", "an", "aT", "aTc", "o", "t1", "mv1", "sd1", "rs1", "n1", "x1b", "xT", "xTc",
                 "h", "hr", "f", "t2", "mv2", "sd2", "rs2", "n2", "y", "mv3", "sd3", "fin")
        (f_rz, f_an, f_aT, f_aTc, f_o, f_t1, f_mv1, f_sd1, f_rs1, f_n1, f_x1b, f_xT, f_xTc,
         f_h, f_hr, f_f, f_t2, f_mv2, f_sd2, f_rs2, f_n2, f_y, f_mv3, f_sd3, f_fin) = (sem("finish_" + n) for n in names)
        f_z, f_g1, f_g2, f_o2, f_nm3 = (sem("finish_" + n) for n in ("z", "g1", "g2", "o2", "nm3"))
        f_bs = [sem(f"finish_bn_stats{n}") for n in range(3)]
        f_rc = [sem(f"finish_reciprocal{n}") for n in range(3)]

        def pairs(k):
            return [E[:, (2 * k + n) * D:(2 * k + n + 1) * D] for n in range(2)]

        an, aT, x1, x1T, x1b, t2 = (pairs(k) for k in range(6))
        xa, xb, outb = ([ring[:, 2 * k + n, :] for n in range(2)] for k in range(3))
        hT = [oh[:, 0, 2 * n:2 * n + 2, :].rearrange("p a w -> p (a w)") for n in range(2)]
        g1, ob, g2, o2, _ = gains
        wo = wq
        zr = est[:, 0:2, 0:HEADS]
        stat = [[est[:, 2 + ln * 2 + n, :] for n in range(2)] for ln in range(3)]
        in_range = lambda t: not isinstance(t, int) or 0 <= t < BLOCKS

        with ExitStack() as banks, nc.Block(no_gpsimd_drain=True) as block:
            pb = lambda name: banks.enter_context(nc.psum_tensor(name, [P, D], f32))
            ps_aT, ps_o, ps_xT, ps_h0, ps_h1, ps_f = (pb(n) for n in ("ps_aT", "ps_o", "ps_xT", "ps_h0", "ps_h1", "ps_f"))
            ps_h = (ps_h0, ps_h1)

            def run(eng, period):
                for k in range(-1, 4):
                    period(k, k % 2)
                with eng.Fori(2, BLOCKS // 2) as i:
                    period(2 * i, 0)
                    period(2 * i + 1, 1)
                for k in range(BLOCKS - 1, BLOCKS + 3):
                    period(k, k % 2)

            @block.sync
            def _(sp):
                def period(k, slot):
                    t = k + 1
                    if in_range(t):
                        p = 1 - slot
                        wait(sp, f_t1, t - 1)
                        sp.dma_start(xa[p], a["x"][ds(t * P, P), :]).then_inc(s_xa[p], 16)
                    t = k - 1
                    if in_range(t):
                        p = 1 - slot
                        wait(sp, f_y, t - 1)
                        sp.dma_start(xb[p], a["x"][ds(t * P, P), :]).then_inc(s_xb[p], 16)
                    t = k - 4
                    if in_range(t) and not (isinstance(t, int) and t == BLOCKS - 1):
                        store(t, slot, P)

                def store(t, p, n):
                    wait(sp, f_fin, t + 1)
                    sp.dma_start(out[ds(t * P, n), :], outb[p][0:n, :]).then_inc(s_st[p], 16)

                run(sp, period)
                store(BLOCKS - 1, 0, NODES - (BLOCKS - 1) * P)
                sp.wait_ge(s_st[0], 16 * (BLOCKS // 2 + 1))
                sp.wait_ge(s_st[1], 16 * (BLOCKS // 2))

            @block.tensor
            def _(pe):
                def period(k, slot):
                    t, p = k - 1, 1 - slot
                    if in_range(t):
                        wait(pe, f_n1, t + 1)
                        wait(pe, f_xTc, t)
                        for c in range(KC):
                            ins = nc.tensor.transpose(ps_xT[:, c * P:(c + 1) * P], x1[p][:, c * P:(c + 1) * P], ident[:])
                        ins.then_inc(f_xT, 1)
                    t, p = k, slot
                    if in_range(t):
                        wait(pe, f_aTc, t + 1)
                        wait(pe, f_t1, t)
                        for c in range(KC):
                            ins = nc.tensor.matmul(ps_o[:], aT[p][:, c * P:(c + 1) * P], wo[:, c, :],
                                                   start=(c == 0), stop=(c == KC - 1))
                        ins.then_inc(f_o, 1)
                    t, p = k - 1, 1 - slot
                    if in_range(t):
                        wait(pe, f_xTc, t + 1)
                        for j in range(FC):
                            wait(pe, f_hr, 2 * t - 1 + j)
                            for c in range(KC):
                                ins = nc.tensor.matmul(ps_h[j][:, 0:P], w1[:, c, j * P:(j + 1) * P],
                                                       x1T[p][:, c * P:(c + 1) * P], start=(c == 0), stop=(c == KC - 1))
                            ins.then_inc(f_h, 1)
                    t, p = k + 1, 1 - slot
                    if in_range(t):
                        wait(pe, f_an, t + 1)
                        wait(pe, f_aTc, t)
                        for c in range(KC):
                            ins = nc.tensor.transpose(ps_aT[:, c * P:(c + 1) * P], an[p][:, c * P:(c + 1) * P], ident[:])
                        ins.then_inc(f_aT, 1)
                    t, p = k - 1, 1 - slot
                    if in_range(t):
                        wait(pe, f_t2, t)
                        for j in range(FC):
                            wait(pe, f_hr, 2 * t + j + 1)
                            ins = nc.tensor.matmul(ps_f[:], hT[p][:, j * P:(j + 1) * P], w2[:, j, :],
                                                   start=(j == 0), stop=(j == FC - 1))
                        ins.then_inc(f_f, 1)

                run(pe, period)

            @block.scalar
            def _(act):
                def root(s, src, done, n):
                    wait(act, src, n)
                    nc.scalar.activation(s[:, 8:9], s[:, 7:8], ACT.Sqrt, bias=eps[:]).then_inc(done, 1)

                def norm(s, x, src, done, n):
                    wait(act, src, n)
                    nc.scalar.activation(x, x, ACT.Identity, scale=s[:, 9:10], bias=s[:, 10:11]).then_inc(done, 1)

                def hidden(t, p, j):
                    wait(act, f_h, 2 * t + j + 1)
                    wait(act, f_f, t - 1)
                    nc.scalar.activation(hT[p][:, j * P:(j + 1) * P], ps_h[j][:, 0:P],
                                         ACT.Relu, bias=b1_col[:, j:j + 1]).then_inc(f_hr, 1)

                def period(k, slot):
                    t, p = k - 1, 1 - slot
                    if in_range(t):
                        wait(act, f_xT, t + 1)
                        wait(act, f_h, 2 * t - 2)
                        nc.scalar.activation(x1T[p], ps_xT[:], ACT.Copy).then_inc(f_xTc, 1)
                    t, p = k - 2, slot
                    if in_range(t):
                        root(stat[1][p], f_mv2, f_sd2, t + 1)
                    if in_range(k - 3):
                        root(stat[2][1 - slot], f_mv3, f_sd3, k - 2)
                    if in_range(t):
                        norm(stat[1][p], t2[p], f_rs2, f_n2, t + 1)
                    if in_range(k - 1):
                        hidden(k - 1, 1 - slot, 0)
                    if in_range(k):
                        root(stat[0][slot], f_mv1, f_sd1, k + 1)
                    if in_range(k - 1):
                        hidden(k - 1, 1 - slot, 1)
                    if in_range(k):
                        norm(stat[0][slot], x1[slot], f_rs1, f_n1, k + 1)
                    t, p = k + 1, 1 - slot
                    if in_range(t):
                        wait(act, f_aT, t + 1)
                        wait(act, f_o, t - 1)
                        nc.scalar.activation(aT[p], ps_aT[:], ACT.Copy).then_inc(f_aTc, 1)

                run(act, period)

            @block.gpsimd
            def _(pool):
                def period(k, slot):
                    t, p = k - 2, slot
                    if in_range(t):
                        wait(pool, f_g2, t + 1)
                        nc.gpsimd.tensor_tensor(t2[p], t2[p], o2, ALU.add).then_inc(f_o2, 1)
                        wait(pool, f_o2, t + 1)
                        wait(pool, s_xb[p], 8 * (t - p) + 16)
                        nc.gpsimd.tensor_tensor(t2[p], t2[p], xb[p], ALU.add).then_inc(f_y, 1)
                    t, p = k, slot
                    if in_range(t):
                        wait(pool, f_n1, t + 1)
                        wait(pool, f_t2, t - 1)
                        nc.gpsimd.tensor_tensor(x1b[p], x1[p], g1, ALU.mult).then_inc(f_g1, 1)
                        wait(pool, f_g1, t + 1)
                        nc.gpsimd.tensor_tensor(x1b[p], x1b[p], ob, ALU.add).then_inc(f_x1b, 1)

                run(pool, period)

            @block.vector
            def _(dve):
                v = nc.vector

                def stats(ln, p, x, ready, n, done):
                    s = stat[ln][p]
                    wait(dve, ready, n)
                    v.bn_stats(s[:, 0:6], x).then_inc(f_bs[ln], 1)
                    wait(dve, f_bs[ln], n)
                    dve.nop(nofuse=True)
                    v.bn_aggr(s[:, 6:8], s[:, 0:6]).then_inc(done, 1)

                def scales(ln, p, ready, n, done):
                    s = stat[ln][p]
                    wait(dve, ready, n)
                    v.reciprocal(s[:, 9:10], s[:, 8:9]).then_inc(f_rc[ln], 1)
                    wait(dve, f_rc[ln], n)
                    v.tensor_scalar(s[:, 10:11], s[:, 6:7], s[:, 9:10], -1.0, ALU.mult, ALU.mult).then_inc(done, 1)

                def period(k, slot):
                    t, p = k - 2, slot
                    if in_range(t):
                        wait(dve, f_f, t + 1)
                        wait(dve, f_x1b, t + 1)
                        wait(dve, f_fin, t - 1)
                        v.tensor_tensor(t2[p], ps_f[:], x1b[p], ALU.add).then_inc(f_t2, 1)
                    t, p = k - 3, 1 - slot
                    if in_range(t):
                        stats(2, p, t2[p], f_y, t + 1, f_mv3)
                    t, p = k - 2, slot
                    if in_range(t):
                        stats(1, p, t2[p], f_t2, t + 1, f_mv2)
                    t, p = k + 1, 1 - slot
                    if in_range(t):
                        z = q_blk[:, ds(t, 1), D:W].rearrange("p a w -> p (a w)")
                        wait(dve, f_an, t - 1)
                        v.tensor_scalar_max(zr[:, p, :], z, 1e-30).then_inc(f_z, 1)
                        wait(dve, f_z, t + 1)
                        v.reciprocal(zr[:, p, :], zr[:, p, :]).then_inc(f_rz, 1)
                    if in_range(k - 3):
                        scales(2, 1 - slot, f_sd3, k - 2, f_nm3)
                    if in_range(k - 2):
                        scales(1, slot, f_sd2, k - 1, f_rs2)
                    if in_range(t):
                        wait(dve, f_rz, t + 1)
                        wait(dve, f_aT, t - 1)
                        v.tensor_tensor(an[p].rearrange("p (h d) -> p h d", h=HEADS),
                                        q_blk[:, ds(t, 1), 0:D].rearrange("p a (h d) -> p (a h) d", h=HEADS),
                                        zr[:, p, :].unsqueeze(2).to_broadcast([P, HEADS, DK]), ALU.mult).then_inc(f_an, 1)
                    t, p = k - 3, 1 - slot
                    if in_range(t):
                        wait(dve, f_nm3, t + 1)
                        wait(dve, s_st[p], 8 * (t - p))
                        v.tensor_scalar(outb[p], t2[p], stat[2][p][:, 9:10], stat[2][p][:, 10:11],
                                        ALU.mult, ALU.add).then_inc(f_fin, 1)
                    t, p = k - 2, slot
                    if in_range(t):
                        wait(dve, f_n2, t + 1)
                        v.tensor_tensor(t2[p], t2[p], g2, ALU.mult).then_inc(f_g2, 1)
                    t, p = k, slot
                    if in_range(t):
                        wait(dve, f_o, t + 1)
                        wait(dve, s_xa[p], 8 * (t - p) + 16)
                        wait(dve, f_g1, t - 1)
                        v.tensor_tensor(x1[p], ps_o[:], xa[p], ALU.add).then_inc(f_t1, 1)
                        stats(0, p, x1[p], f_t1, t + 1, f_mv1)
                        scales(0, p, f_sd1, t + 1, f_rs1)

                run(dve, period)


def kernel(**inputs):
    import numpy as np
    import concourse.bacc as bacc
    from concourse.bass_utils import run_bass_kernel_spmd

    g = {k.replace("L0_gnn_", ""): np.asarray(v) for k, v in inputs.items()}
    x = np.zeros((XT * P, D), g["x"].dtype)
    x[:NODES] = g["x"]
    n = TILES * P
    edges = np.zeros((3, n), g["src"].dtype)
    edges[0, :EDGES] = g["src"]
    edges[1, :] = BLOCKS * P - 1
    edges[1, :EDGES] = g["dst"]
    edges[2, 0] = -1
    edges[2, 1:] = edges[1, :-1]
    arrays = {
        "x": x,
        "xt": np.ascontiguousarray(x.reshape(XT, P, KC, P).transpose(0, 3, 2, 1)),
        "edges": np.ascontiguousarray(edges.reshape(3, TILES, P).transpose(1, 0, 2)).reshape(TILES, 3 * P),
        "tile_last": np.ascontiguousarray(edges[1].reshape(TILES, P)[:, -1]).reshape(1, TILES),
        "g1_col": np.ascontiguousarray(g["ln1_g"].reshape(KC, P).T),
        "o1_col": np.ascontiguousarray(g["ln1_b"].reshape(KC, P).T),
        "b1": np.ascontiguousarray(g["b1"].reshape(FC, P).T),
    }
    for name in ("Wq", "Wk", "Wv", "Wo", "W1", "W2"):
        w = g[name]
        arrays[name.lower()] = np.ascontiguousarray(w.reshape(w.shape[0] // P, P, w.shape[1]).transpose(1, 0, 2))
    for name in ("ln1_g", "ln1_b", "ln2_g", "ln2_b", "b2"):
        arrays[name] = g[name].reshape(1, D)
    nc = bacc.Bacc("TRN2", target_bir_lowering=False, num_devices=1)
    aps = {k: nc.dram_tensor("in_" + k, v.shape, mybir.dt.from_np(v.dtype), kind="ExternalInput").ap()
           for k, v in arrays.items()}
    out = nc.dram_tensor("out_0", (NODES, D), mybir.dt.float32, kind="ExternalOutput").ap()
    program(nc, aps, out)
    r = run_bass_kernel_spmd(nc, [{"in_" + k: v for k, v in arrays.items()}], core_ids=[0])
    return r.results[0]["out_0"]
```

```python
import concourse.bass as bass
from concourse import mybir
from contextlib import ExitStack

P = 128
NODES, EDGES, D, HEADS, DFF = 6250, 100000, 512, 8, 256
DK = D // HEADS
KC = D // P
FC = DFF // P
BLOCKS = -(-NODES // P)
TILES = 8 * -(-EDGES // (8 * P))
UN = 16
STEPS = 2 * UN * -(-(-(-EDGES // P) + BLOCKS - 1) // (2 * UN))
RUNS = P // HEADS
RL = STEPS // RUNS
RE = RL * P
GROUPS = -(-STEPS // P)
TROWS = GROUPS * P
XT = RL
DZ = DK + 1
W = HEADS * DZ
RING = 8
SKIP = 20000
BIG = 2.0 ** 126
EPS = 1e-5
SUM_HEADS = 4
MUL_HEADS = 4


def program(nc, a, out):
    f32, bf16, i32 = mybir.dt.float32, mybir.dt.bfloat16, mybir.dt.int32
    ALU, ACT, AX = mybir.AluOpType, mybir.ActivationFunctionType, mybir.AxisListType
    ds = bass.ds
    ctx = ExitStack()

    def sb(name, shape, dt=f32):
        return ctx.enter_context(nc.sbuf_tensor(name, shape, dt))

    def sem(name):
        return ctx.enter_context(nc.semaphore(name))

    def wait(eng, s, n):
        if not isinstance(n, int) or n > 0:
            eng.wait_ge(s, n)
            if eng is nc.gpsimd and not isinstance(n, int):
                eng.nop(nofuse=True)

    def repeat(eng, n, body, start=0):
        body(start)
        with eng.Fori(start + 1, n) as i:
            body(i)

    def load8(eng, regs, table, at):
        eng.load(regs, table[0:1, ds(at, 8)])
        return [eng.snap(r, min_val=0, max_val=BLOCKS - 1) for r in regs]

    def dram(name, shape, dt):
        return nc.dram_tensor(name, shape, dt, kind="Internal").ap()

    k_tab = dram("k_tab", (BLOCKS * P, D), f32)
    v_tab = dram("v_tab", (RL * P, W), f32)
    seg_d = dram("seg_d", (TROWS * P,), bf16)
    loc_d = dram("loc_d", (TROWS * P,), bf16)
    blk_d = dram("blk_d", (TROWS,), i32)

    with ctx:
        R = sb("R", [P, BLOCKS * W])
        E = sb("E", [P, (RL + 1) * P])
        wq = sb("wq", [P, KC, D])
        wv = sb("wv", [P, KC, D])
        w1 = sb("w1", [P, KC, DFF])
        w2 = sb("w2", [P, FC, D])
        ring = sb("ring", [P, RING, W])
        prod = sb("prod", [P, 4, W])
        oh = sb("oh", [P, 2, 8, P])
        loc = sb("loc", [P, 2, 8 * P], bf16)
        xt = sb("xt", [P, 2, KC, P])
        vout = sb("vout", [P, W])
        src_t = sb("src_t", [P, TROWS], i32)
        loc_t = sb("loc_t", [P, TROWS], bf16)
        inv_t = sb("inv_t", [P, TROWS], bf16)
        blk_steps = sb("blk_steps", [1, STEPS], i32)
        blk_cols = sb("blk_cols", [1, STEPS], i32)
        idx = sb("idx", [P, 2, UN], i32)
        ident = sb("ident", [P, P])
        iota_row = sb("iota_row", [P, P], bf16)
        iota_col = sb("iota_col", [P, 1])
        one = sb("one", [1, 1])
        b1_col = sb("b1_col", [P, FC])
        g1_col = sb("g1_col", [P, KC])
        o1_col = sb("o1_col", [P, KC])
        eps = sb("eps", [P, 1])
        est = sb("est", [P, HEADS, UN])

        q_blk = R[:, :].rearrange("p (b w) -> p b w", w=W)
        wk = ring[:, 0:KC, 0:D]
        e_all = E[:, 0:HEADS * STEPS].rearrange("p (h s) -> p h s", h=HEADS)

        s_wk = sem("wk_in")
        s_w2, s_pc = sem("weights_in"), sem("pool_constants")
        s_wq = [sem(f"wq_in{c}") for c in range(KC)]
        s_x = [sem(f"xt_in{i}") for i in range(2)]
        s_qps, s_kps = sem("q_product_done"), sem("k_product_done")
        s_qout, s_kout = sem("q_copied"), sem("k_copied")
        s_kst = [sem(f"k_stored{i}") for i in range(2)]
        s_tin, s_const = sem("table_inputs_in"), sem("constants_ready")
        s_tidx, s_tg = sem("tile_index_ready"), sem("edge_rows_in")
        s_tT, s_tTc = sem("table_transposed"), sem("table_copied")
        s_rows, s_tst, s_tld = sem("table_rows_ready"), sem("table_rows_stored"), sem("block_rows_in")
        s_dc = sem("vector_chain")
        chain = [0]

        def link(dve, ins):
            chain[0] += 1
            ins.then_inc(s_dc, 1)
            dve.wait_ge(s_dc, chain[0])

        TB = 34 * W
        N3 = GROUPS * P

        def tmp(n, cols=N3):
            return R[:, TB + n * N3:TB + n * N3 + cols]

        last_i, lastf, key = (E[:, i * TILES:(i + 1) * TILES] for i in range(3))
        rows_i = tmp(0, 3 * N3).bitcast(i32).rearrange("p (g w) -> p g w", g=GROUPS)
        dstf = tmp(3).rearrange("p (g w) -> p g w", g=GROUPS)
        prevf = tmp(4).rearrange("p (g w) -> p g w", g=GROUPS)
        srcf = tmp(5).rearrange("p (g w) -> p g w", g=GROUPS)
        valid = tmp(6).rearrange("p (g w) -> p g w", g=GROUPS)
        packed = tmp(7, N3).bitcast(bf16).rearrange("p (k g w) -> p k g w", k=2, g=GROUPS)
        small = E[:, 3 * TILES:3 * TILES + 64]
        scol, tstep, bstep, base = (small[:, i * 8:i * 8 + GROUPS] for i in range(4))
        scol_i, tstep_i, bstep_i = (small[:, 32 + i * 8:32 + i * 8 + GROUPS].bitcast(i32) for i in range(3))
        iota_t = E[:, 4 * TILES:5 * TILES]
        iota_ti = E[:, 5 * TILES:6 * TILES].bitcast(i32)
        iota_ri = E[:, 6 * TILES:6 * TILES + P].bitcast(i32)
        iota_ci = E[:, 6 * TILES + P:6 * TILES + P + 1].bitcast(i32)

        kout = prod[:, 0:2, 0:D]
        x_tile = lambda t: a["xt"][ds(t, 1)].rearrange("a p k n -> p (a k) n")

        s_idx = [sem(f"k_index_columns_in{i}") for i in range(2)]
        s_loc = [sem(f"loc_in{i}") for i in range(2)]
        s_xv = sem("xt_for_v_in")

        def load_loc(sp, n, half):
            sp.dma_start(loc[:, half], loc_d[ds(n * 8 * P, 8 * P)].rearrange("(a w) -> a w", a=1)
                         .to_broadcast([P, 8 * P])).then_inc(s_loc[half], 16)

        def load_idx(sp, group, par):
            sp.dma_start(idx[:, par, :], src_t[:, ds(group * UN, UN)]).then_inc(s_idx[par], 16)

        with nc.psum_tensor("ps_q", [P, 2, D], f32) as ps_q, \
                nc.psum_tensor("ps_k", [P, 2, D], f32) as ps_k, \
                nc.psum_tensor("ps_t", [P, 2, D], f32) as ps_t, nc.Block(no_gpsimd_drain=True) as block:

            @block.sync
            def _(sp):
                def load(t, slot):
                    wait(sp, s_kps, t - 1)
                    sp.dma_start(xt[:, slot], x_tile(t)).then_inc(s_x[slot], 16)

                def store(t, slot):
                    wait(sp, s_kout, t + 1)
                    sp.dma_start(k_tab[ds(t * P, P), :], kout[:, slot]).then_inc(s_kst[slot], 16)

                def pair(i):
                    for slot in range(2):
                        t = 2 * i + slot
                        load(t, slot)
                        if isinstance(t, int) and t == 0:
                            for c in range(KC):
                                sp.dma_start(wq[:, c], a["wq"][:, c]).then_inc(s_wq[c], 16)
                            sp.dma_start(last_i.bitcast(i32), a["tile_last"][0:1, :].to_broadcast([P, TILES])).then_inc(s_tin, 16)
                            sp.dma_start(wk, a["wk"]).then_inc(s_wk, 16)
                        if isinstance(t, int) and t == 1:
                            sp.dma_start(wv[:], a["wv"]).then_inc(s_w2, 16)
                            sp.dma_start(w1[:], a["w1"]).then_inc(s_w2, 16)
                            sp.dma_start(w2[:], a["w2"]).then_inc(s_w2, 16)
                        if not (isinstance(t, int) and t == 0):
                            store(t - 1, 1 - slot)

                pair(0)
                with sp.Fori(1, 8) as i:
                    pair(i)
                sp.wait_ge(s_rows, 1)
                for n, t in enumerate((seg_d, loc_d)):
                    sp.dma_start(t.rearrange("(g p w) -> p g w", p=P, w=P), packed[:, n]).then_inc(s_tst, 16)
                with nc.allow_non_contiguous_dma(reason="896 block numbers, once"):
                    sp.dma_start(blk_d.rearrange("(g p) -> p g", p=P), bstep_i).then_inc(s_tst, 16)
                    sp.wait_ge(s_tst, 48)
                    sp.dma_start(blk_steps[:], blk_d[0:STEPS].rearrange("(a s) -> a s", a=1)).then_inc(s_tld, 16)
                    sp.dma_start(blk_cols[:].rearrange("a (c j) -> a c j", j=RUNS),
                                 blk_d[0:STEPS].rearrange("(a j c) -> a c j", a=1, j=RUNS)).then_inc(s_tld, 16)
                with sp.Fori(8, BLOCKS // 2) as i:
                    pair(i)
                load(BLOCKS - 1, 0)
                sp.wait_ge(s_tTc, 2 * GROUPS)
                for par in range(2):
                    load_idx(sp, par, par)
                    load_loc(sp, par, par)
                sp.wait_ge(s_kps, BLOCKS - 1)
                sp.dma_start(xt[:, 1], x_tile(0)).then_inc(s_xv, 16)
                store(BLOCKS - 2, 1)
                store(BLOCKS - 1, 0)
                sp.wait_ge(s_w2, 48)
                sp.wait_ge(s_tld, 32)
                sp.wait_ge(s_kst[0], 16 * (BLOCKS // 2 + 1))
                sp.wait_ge(s_kst[1], 16 * (BLOCKS // 2))

            @block.tensor
            def _(pe):
                def tile(i, slot):
                    t = 2 * i + slot
                    wait(pe, s_x[slot], 16 * (i + 1))
                    wait(pe, s_qout, t - 1)
                    wait(pe, s_kout, t - 1)
                    for ps, w, done in ((ps_q, wq, s_qps), (ps_k, wk, s_kps)):
                        if isinstance(t, int) and t == 0 and w is wk:
                            pe.wait_ge(s_wk, 16)
                        for c in range(KC):
                            if isinstance(t, int) and t == 0 and w is wq:
                                pe.wait_ge(s_wq[c], 16)
                            last = nc.tensor.matmul(ps[:, slot, :], xt[:, slot, c, :], w[:, c, :],
                                                    start=(c == 0), stop=(c == KC - 1))
                        last.then_inc(done, 1)

                def pair(i):
                    tile(i, 0)
                    tile(i, 1)

                pair(0)
                with pe.Fori(1, 8) as i:
                    pair(i)
                pe.wait_ge(s_const, 1)
                pe.wait_ge(s_rows, 1)
                for g in range(GROUPS):
                    for n, what in ((0, srcf), (1, dstf)):
                        wait(pe, s_tTc, 2 * g + n - 1)
                        nc.tensor.transpose(ps_t[:, n, 0:P], what[:, g, :], ident[:]).then_inc(s_tT, 1)
                with pe.Fori(8, BLOCKS // 2) as i:
                    pair(i)
                tile(BLOCKS // 2, 0)

            @block.scalar
            def _(act):
                def tile(i, slot):
                    t = 2 * i + slot
                    wait(act, s_qps, t + 1)
                    nc.scalar.activation(q_blk[:, ds(t, 1), 0:D].rearrange("p a w -> p (a w)"),
                                         ps_q[:, slot, :], ACT.Copy).then_inc(s_qout, 1)
                    wait(act, s_kps, t + 1)
                    wait(act, s_kst[slot], 16 * i)
                    nc.scalar.activation(kout[:, slot, :], ps_k[:, slot, :], ACT.Copy).then_inc(s_kout, 1)

                def pair(i):
                    tile(i, 0)
                    tile(i, 1)

                pair(0)
                with act.Fori(1, 12) as i:
                    pair(i)
                act.wait_ge(s_tTc, 2 * GROUPS)
                act.wait_ge(s_tst, 48)
                with act.Fori(12, BLOCKS // 2) as i:
                    pair(i)
                tile(BLOCKS // 2, 0)

            @block.gpsimd
            def _(pool):
                nc.gpsimd.memset(ident[:], 0.0).then_inc(s_pc, 1)
                nc.gpsimd.iota(iota_ti, [[1, TILES]], base=0, channel_multiplier=0).then_inc(s_pc, 1)
                nc.gpsimd.iota(scol_i, [[P, GROUPS]], base=0, channel_multiplier=1).then_inc(s_pc, 1)
                nc.gpsimd.iota(iota_ri, [[1, P]], base=0, channel_multiplier=0).then_inc(s_pc, 1)
                nc.gpsimd.iota(iota_ci, [[0, 1]], base=0, channel_multiplier=1).then_inc(s_pc, 1)
                nc.gpsimd.memset(one[:], 1.0).then_inc(s_pc, 1)
                nc.gpsimd.memset(ring[:, KC:RING, :], 0.0)
                nc.gpsimd.memset(ring[:, 0:KC, D:W], 0.0)
                nc.gpsimd.memset(vout[:], 1.0)
                nc.gpsimd.memset(eps[:], EPS)
                pool.wait_ge(s_pc, 1)
                nc.gpsimd.affine_select(out=ident[:], in_=ident[:], compare_op=ALU.not_equal, fill=1.0,
                                        base=0, pattern=[[-1, P]], channel_multiplier=1).then_inc(s_const, 1)
                pool.wait_ge(s_tidx, 1)
                for g in range(GROUPS):
                    pool.indirect_dma_start(out=rows_i[:, g, :], out_offset=None, in_=a["edges"],
                                            in_offset=bass.IndirectOffsetOnAxis(ap=tstep_i[:, g:g + 1], axis=0),
                                            bounds_check=TILES - 1, oob_is_err=False).then_inc(s_tg, 16)
                pool.wait_ge(s_tg, 16 * GROUPS)

            @block.vector
            def _(dve):
                v = nc.vector
                dve.wait_ge(s_tin, 16)
                dve.wait_ge(s_pc, 6)
                v.tensor_copy(iota_row[:], iota_ri)
                v.tensor_copy(iota_col[:], iota_ci)
                v.tensor_copy(scol, scol_i)
                v.tensor_copy(iota_t, iota_ti)
                link(dve, v.tensor_single_scalar(last_i.bitcast(i32), last_i.bitcast(i32), 7, ALU.arith_shift_right))
                link(dve, v.tensor_copy(lastf, last_i.bitcast(i32)))
                link(dve, v.tensor_tensor(key, lastf, iota_t, ALU.add))
                for g in range(GROUPS):
                    link(dve, v.tensor_scalar(lastf, key, scol[:, g:g + 1], 0.0, ALU.is_lt, ALU.add,
                                              accum_out=tstep[:, g:g + 1]))
                link(dve, v.tensor_scalar_min(tstep, tstep, float(TILES - 1)))
                v.tensor_copy(tstep_i, tstep).then_inc(s_tidx, 1)
                link(dve, v.tensor_tensor(bstep, scol, tstep, ALU.subtract))
                link(dve, v.tensor_copy(bstep_i, bstep))
                link(dve, v.tensor_scalar_mul(base, bstep, float(P)))
                dve.wait_ge(s_tg, 16 * GROUPS)
                v.tensor_copy(srcf, rows_i[:, :, 0:P])
                v.tensor_copy(prevf, rows_i[:, :, 2 * P:3 * P])
                link(dve, v.tensor_copy(dstf, rows_i[:, :, P:2 * P]))
                link(dve, v.tensor_tensor(prevf, dstf, prevf, ALU.not_equal))
                for g in range(GROUPS):
                    ins = v.tensor_scalar(dstf[:, g, :], dstf[:, g, :], base[:, g:g + 1], None, ALU.subtract)
                link(dve, ins)
                link(dve, v.tensor_scalar(valid, dstf, 0.0, None, ALU.is_ge))
                link(dve, v.scalar_tensor_tensor(valid, dstf, float(P - 1), valid, ALU.is_le, ALU.mult))
                v.scalar_tensor_tensor(packed[:, 0], prevf, -BIG, valid, ALU.mult, ALU.mult)
                link(dve, v.scalar_tensor_tensor(dstf, dstf, -255.0, valid, ALU.add, ALU.mult))
                link(dve, v.tensor_scalar_add(dstf, dstf, 255.0))
                link(dve, v.tensor_copy(packed[:, 1], dstf))
                link(dve, v.tensor_scalar(valid, valid, -float(SKIP), float(SKIP), ALU.mult, ALU.add))
                v.tensor_tensor(srcf, srcf, valid, ALU.add).then_inc(s_rows, 1)
                for g in range(GROUPS):
                    for n, to in ((0, src_t), (1, loc_t)):
                        dve.wait_ge(s_tT, 2 * g + n + 1)
                        v.tensor_copy(to[:, g * P:(g + 1) * P], ps_t[:, n, 0:P]).then_inc(s_tTc, 1)
                dve.wait_ge(s_tTc, 2 * GROUPS)
                link(dve, v.tensor_scalar(inv_t[:], loc_t[:], float(P), -BIG, ALU.is_ge, ALU.mult))

        s_k = [sem(f"k_rows_in{i}") for i in range(RING)]
        s_oh, s_qx, s_mul, s_sum = sem("onehot_ready"), sem("q_expanded"), sem("product_ready"), sem("scalar_heads_summed")
        s_red, s_vps, s_vout, s_vst = (sem(n) for n in ("vector_heads_summed", "v_product_done", "v_copied", "v_stored"))
        s_mc = sem("scores_moved")

        with nc.psum_tensor("ps_qx", [P, 4, D], f32) as ps_qx, \
                nc.psum_tensor("ps_v", [P, D], f32) as ps_v, nc.Block(no_gpsimd_drain=True) as block:

            @block.sync
            def _(sp):
                def body(i):
                    for par in range(2):
                        g = 2 * i + par
                        for half in range(2):
                            n = 2 * g + 2 + half
                            wait(sp, s_oh, n - 1)
                            load_loc(sp, n, half)
                        wait(sp, s_vout, g + 1)
                        sp.dma_start(v_tab[ds(g * P, P), :], vout[:]).then_inc(s_vst, 16)
                        if not (isinstance(g, int) and g == RL - 1):
                            sp.dma_start(xt[:, 1], x_tile(g + 1)).then_inc(s_xv, 16)
                        if not (isinstance(g, int) and g >= RL - 2):
                            wait(sp, s_mul, UN * (g + 1))
                            load_idx(sp, g + 2, par)

                repeat(sp, RL // 2 - 1, body)
                body(RL // 2 - 1)
                for half in range(2):
                    sp.wait_ge(s_loc[half], 16 * (RL + 1))

            @block.gpsimd
            def _(pool):
                bound = pool.to_reg(BLOCKS * P - 1)

                def body(i):
                    for par in range(2):
                        wait(pool, s_idx[par], 16 * (i + 1))
                        for u in range(UN):
                            s = UN * (2 * i + par) + u
                            wait(pool, s_mul, s - 7)
                            pool.indirect_dma_start(out=ring[:, u % RING, 0:D], out_offset=None, in_=k_tab,
                                                    in_offset=bass.IndirectOffsetOnAxis(ap=idx[:, par, u:u + 1], axis=0),
                                                    bounds_check=bound, oob_is_err=False).then_inc(s_k[u % RING], 16)

                repeat(pool, RL // 2, body)

            @block.tensor
            def _(pe):
                regs = [pe.alloc_register(f"pe_blk{u}") for u in range(8)]

                def body(i):
                    for half in range(2):
                        blk = load8(pe, regs, blk_steps, UN * i + 8 * half)
                        wait(pe, s_oh, 2 * i + half + 1)
                        for u in range(8):
                            s = UN * i + 8 * half + u
                            wait(pe, s_mul, s - 3)
                            nc.tensor.matmul(ps_qx[:, u % 4, :], oh[:, half, u, :],
                                             q_blk[:, ds(blk[u], 1), 0:D].rearrange("p a w -> p (a w)"),
                                             start=True, stop=True).then_inc(s_qx, 1)
                            if half and u % 2:
                                c = u // 2
                                if c == 0:
                                    wait(pe, s_xv, 16 * (i + 1))
                                last = nc.tensor.matmul(ps_v[:], xt[:, 1, c, :], wv[:, c, :],
                                                        start=(c == 0), stop=(c == KC - 1))
                                if c == KC - 1:
                                    last.then_inc(s_vps, 1)

                repeat(pe, RL, body)

            @block.vector
            def _(dve):
                def build(n, half):
                    wait(dve, s_loc[half], 16 * ((n - half) // 2 + 1) if isinstance(n, int) else 8 * (n - half) + 16)
                    wait(dve, s_qx, 8 * (n - 1))
                    nc.vector.tensor_scalar(oh[:, half].rearrange("p u w -> p (u w)"), loc[:, half],
                                            iota_col[:, 0:1], None, ALU.is_equal).then_inc(s_oh, 1)

                build(0, 0)

                def body(i):
                    for u in range(UN):
                        s = UN * i + u
                        if u == 4:
                            build(2 * i + 1, 1)
                        if u == 12:
                            build(2 * i + 2, 0)
                        wait(dve, s_qx, s + 1)
                        wait(dve, s_k[u % 8], 32 * i + 16 * (u // 8 + 1))
                        wait(dve, s_sum, s - 3)
                        nc.vector.tensor_tensor(prod[:, u % 4, 0:D], ps_qx[:, u % 4, :], ring[:, u % 8, 0:D],
                                                ALU.mult).then_inc(s_mul, 1)
                        if not (isinstance(s, int) and s == 0):
                            sums(s - 1, (u - 1) % UN)
                        if u == 10:
                            move(2 * i, 0)
                        if u == 2 and not isinstance(i, int):
                            move(2 * i - 1, 1)

                def sums(s, u):
                    wait(dve, s_mul, s + 1)
                    nc.vector.tensor_reduce(est[:, 0:SUM_HEADS, u], prod[:, u % 4, 0:SUM_HEADS * DK]
                                            .rearrange("p (h d) -> p h d", h=SUM_HEADS), AX.X, ALU.add).then_inc(s_red, 1)

                def move(n, half):
                    wait(dve, s_red, 8 * n + 8)
                    wait(dve, s_sum, 8 * n + 8)
                    nc.vector.tensor_tensor(e_all[:, :, ds(8 * n, 8)], est[:, :, 8 * half:8 * half + 8],
                                            inv_t[:, ds(8 * n, 8)].unsqueeze(1).to_broadcast([P, HEADS, 8]),
                                            ALU.add).then_inc(s_mc, 1)

                repeat(dve, RL, body)
                sums(STEPS - 1, UN - 1)
                move(2 * RL - 1, 1)

            @block.scalar
            def _(act):
                def body(i):
                    for u in range(UN):
                        s = UN * i + u
                        wait(act, s_mul, s + 1)
                        wait(act, s_mc, 2 * i - 1 + u // 8)
                        for h in range(SUM_HEADS, HEADS):
                            part = prod[:, u % 4, h * DK:(h + 1) * DK]
                            ins = nc.scalar.activation(part, part, ACT.Copy,
                                                       accum_out=est[:, h, u:u + 1])
                        ins.then_inc(s_sum, 1)
                    wait(act, s_vps, i + 1)
                    wait(act, s_vst, 16 * i)
                    nc.scalar.activation(vout[:].rearrange("p (h d) -> p h d", h=HEADS)[:, :, 0:DK],
                                         ps_v[:].rearrange("p (h d) -> p h d", h=HEADS), ACT.Copy).then_inc(s_vout, 1)

                repeat(act, RL, body)

        s_mi = sem("masks_in")
        s_sc, s_eT, s_eM = sem("scores_staged"), sem("scores_transposed"), sem("scores_masked")
        s_col, s_colT, s_row, s_rowT = sem("ends_ready"), sem("ends_transposed"), sem("carries_ready"), sem("carries_transposed")
        s_wc, s_bp = sem("columns_in"), sem("folded_bias_product")
        s_max, s_any = sem("maxima_done"), sem("starts_summed")
        s_dead, s_zero, s_wo = sem("maxima_used"), sem("sums_cleared"), sem("late_weights_in")

        sc_t = R[:, 0:RE]
        mx_t = R[:, RE:2 * RE]
        seg_t = R[:, 2 * RE:2 * RE + RE // 2 + 2].bitcast(bf16)
        work_end = 2 * RE + RE // 2 + 2
        stage = prod[:, 0:2, 0:D]
        cols = est[:, 0, 0:8]
        rows = oh[0:1, 0, :, :]
        e_runs = e_all.rearrange("p h (j c) -> p c h j", c=RL)

        def units(eng, unit):
            def pair(i):
                unit(2 * i, 0)
                unit(2 * i + 1, 1)
            repeat(eng, RL // 8, pair)
            unit(RL // 4 - 1, 0)

        gains = [wv[:, c, :] for c in range(4)] + [vout[:, 0:D]]

        cut = 4352
        z1, z2 = 3800, 8600

        s_v = [sem(f"v_rows_in{i}") for i in range(RING)]
        s_vidx = [sem(f"v_index_columns_in{i}") for i in range(2)]
        s_order = sem("index_table_reordered")
        src_c = xt[:].rearrange("p a k n -> p (a k n)")[:, 0:STEPS].bitcast(i32)

        def load_vidx(sp, c, par):
            sp.dma_start(idx[:, par, :], src_c[:, ds(c * RUNS, RUNS)]).then_inc(s_vidx[par], 16)

        def gather(pool, i, par, j, bound):
            s = UN * (2 * i + par) + j
            if j == 0:
                wait(pool, s_vidx[par], 16 * (i + 1))
            wait(pool, s_wd, s - 7)
            wait(pool, s_wa, s - 7)
            pool.indirect_dma_start(out=ring[:, j % RING, :], out_offset=None, in_=v_tab,
                                    in_offset=bass.IndirectOffsetOnAxis(ap=idx[:, par, j:j + 1], axis=0),
                                    bounds_check=bound, oob_is_err=False).then_inc(s_v[j % RING], 16)

        s_wd, s_wa = sem("vector_heads_weighted"), sem("scalar_heads_weighted")

        with nc.psum_tensor("ps_e", [P, 2, D], f32) as ps_e, \
                nc.psum_tensor("ps_c", [P, 2, D], f32) as ps_c, \
                nc.psum_tensor("ps_b", [P, D], f32) as ps_b, nc.Block(no_gpsimd_drain=True) as block:

            @block.sync
            def _(sp):
                for h in range(HEADS):
                    at = slice(h * RUNS, (h + 1) * RUNS)
                    sp.dma_start(seg_t[at, 0:RE], seg_d[0:RUNS * RE].rearrange("(j w) -> j w", j=RUNS)).then_inc(s_mi, 16)
                    with nc.allow_non_contiguous_dma(reason="the first slot of the next run, 16 values"):
                        sp.dma_start(seg_t[at, RE:RE + 1], seg_d[RE:(RUNS + 1) * RE].rearrange("(j w) -> j w", j=RUNS)[:, 0:1]).then_inc(s_mi, 16)
                sp.wait_ge(s_order, 1)
                for par in range(2):
                    load_vidx(sp, par, par)
                sp.dma_start(wq[:], a["wo"]).then_inc(s_wo, 16)
                sp.wait_ge(s_vst, 16 * RL)
                for name, to in zip(("ln1_g", "ln1_b", "ln2_g", "ln2_b", "b2"), gains):
                    sp.dma_start(to, a[name].to_broadcast([P, D])).then_inc(s_wo, 16)
                for name, to in (("b1", b1_col), ("g1_col", g1_col), ("o1_col", o1_col)):
                    sp.dma_start(to[:], a[name]).then_inc(s_wc, 16)
                sp.wait_ge(s_wc, 48)
                sp.wait_ge(s_mi, 16 * 2 * HEADS)
                sp.wait_ge(s_wo, 16 * 6)

            @block.scalar
            def _(act):
                def unit(n, slot):
                    wait(act, s_eT, n - 1)
                    nc.scalar.activation(stage[:, slot, :].rearrange("p (c h j) -> p c h j", c=4, h=HEADS),
                                         e_runs[:, ds(4 * n, 4), :, :], ACT.Copy).then_inc(s_sc, 1)

                units(act, unit)
                act.wait_ge(s_mi, 16 * 2 * HEADS)
                for way in range(2):
                    nc.scalar.activation(R[:, work_end:work_end + RE], seg_t[:, way:RE + way], ACT.Copy, scale=2.0 ** -20,
                                         accum_out=cols[:, 2 * way + 1:2 * way + 2]).then_inc(s_any, 1)
                    act.wait_ge(s_any, way + 1)
                act.wait_ge(s_bp, 1)
                for j in range(FC):
                    nc.scalar.activation(b1_col[:, j:j + 1], ps_b[:, j:j + 1], ACT.Identity, bias=b1_col[:, j:j + 1])
                for c in range(KC):
                    nc.scalar.activation(w1[:, c, :], w1[:, c, :], ACT.Copy, scale=g1_col[:, c:c + 1])
                act.wait_ge(s_max, 1)
                nc.scalar.activation(R[:, 2 * RE:work_end], sc_t[:, 0:work_end - 2 * RE], ACT.Copy, scale=0.0).then_inc(s_dead, 1)
                act.wait_ge(s_dead, 3)
                nc.scalar.activation(R[:, z1:z2], E[:, 0:z2 - z1], ACT.Copy, scale=0.0).then_inc(s_zero, 1)

            @block.tensor
            def _(pe):
                def unit(n, slot):
                    wait(pe, s_sc, n + 1)
                    wait(pe, s_eM, n - 1)
                    for c in range(4):
                        ins = nc.tensor.transpose(ps_e[:, slot, c * P:(c + 1) * P],
                                                  stage[:, slot, c * P:(c + 1) * P], ident[:])
                    ins.then_inc(s_eT, 1)

                units(pe, unit)
                for way in range(2):
                    pe.wait_ge(s_col, way + 1)
                    for n in range(2):
                        ins = nc.tensor.transpose(ps_c[0:1, 0, n * P:(n + 1) * P], cols[:, 2 * way + n:2 * way + n + 1], ident[:])
                    ins.then_inc(s_colT, 1)
                    pe.wait_ge(s_row, way + 1)
                    nc.tensor.matmul(ps_c[:, 1, 0:1], rows[0:1, 4 * way + 3, :], one[0:1, 0:1],
                                     start=True, stop=True).then_inc(s_rowT, 1)
                    if way == 0:
                        pe.wait_ge(s_wc, 48)
                        for j in range(FC):
                            for c in range(KC):
                                ins = nc.tensor.matmul(ps_b[:, j:j + 1], w1[:, c, j * P:(j + 1) * P], o1_col[:, c:c + 1],
                                                       start=(c == 0), stop=(c == KC - 1))
                        ins.then_inc(s_bp, 1)

            @block.gpsimd
            def _(pool):
                nc.gpsimd.tensor_copy(src_c.rearrange("p (c j) -> p c j", j=RUNS),
                                      src_t[:, 0:STEPS].rearrange("p (j c) -> p c j", c=RL)).then_inc(s_order, 1)
                pool.wait_ge(s_vst, 16 * RL)
                for j in range(RING):
                    gather(pool, 0, 0, j, BLOCKS * P - 1)
                pool.wait_ge(s_any, 2)
                nc.gpsimd.memset(R[:, work_end:BLOCKS * W], 0.0).then_inc(s_zero, 1)
                pool.wait_ge(s_wo, 16 * 6)
                nc.gpsimd.tensor_tensor(gains[1], gains[1], gains[4], ALU.add)
                pool.wait_ge(s_max, 1)
                nc.gpsimd.tensor_tensor(E[:, cut:RE], sc_t[:, cut:RE], mx_t[:, cut:RE], ALU.subtract).then_inc(s_dead, 1)
                pool.wait_ge(s_dead, 3)
                nc.gpsimd.memset(R[:, z2:2 * RE], 0.0).then_inc(s_zero, 1)

            @block.vector
            def _(dve):
                v = nc.vector
                def unit(n, slot):
                    wait(dve, s_eT, n + 1)
                    v.tensor_copy(sc_t[:, ds(4 * P * n, 4 * P)], ps_e[:, slot, :]).then_inc(s_eM, 1)

                units(dve, unit)
                dve.wait_ge(s_eM, RL // 4)
                dve.wait_ge(s_mi, 16 * 2 * HEADS)

                for way, (reset, data) in enumerate(((seg_t[:, 0:RE], sc_t),
                                                         (seg_t[:, RE:0:-1], mx_t[:, ::-1]))):
                    end = RE - 1 if way == 0 else 0
                    trial = E[:, 0:RE] if way == 0 else E[:, 0:RE][:, ::-1]
                    link(dve, v.tensor_tensor_scan(trial, reset, data, -BIG, ALU.add, ALU.max))
                    v.tensor_copy(cols[:, 2 * way:2 * way + 1], E[:, end:end + 1])
                    dve.wait_ge(s_any, way + 1)
                    v.tensor_scalar(cols[:, 2 * way + 1:2 * way + 2], cols[:, 2 * way + 1:2 * way + 2],
                                    0.0, -BIG, ALU.is_lt, ALU.mult).then_inc(s_col, 1)
                    dve.wait_ge(s_colT, way + 1)
                    got, res, inc, carry = (rows[0:1, 4 * way + n, :] for n in range(4))
                    heads = lambda r: r.rearrange("a (h j) -> a h j", h=HEADS)
                    v.tensor_copy(got, ps_c[0:1, 0, 0:P])
                    link(dve, v.tensor_copy(res, ps_c[0:1, 0, P:2 * P]))
                    first = 0 if way == 0 else RUNS - 1
                    v.memset(carry, -BIG)
                    link(dve, v.memset(heads(res)[:, :, first:first + 1], -BIG))
                    if way == 0:
                        link(dve, v.tensor_tensor_scan(inc, res, got, -BIG, ALU.add, ALU.max))
                        v.tensor_copy(heads(carry)[:, :, 1:RUNS], heads(inc)[:, :, 0:RUNS - 1]).then_inc(s_row, 1)
                    else:
                        link(dve, v.tensor_tensor_scan(inc[:, ::-1], res[:, ::-1], got[:, ::-1], -BIG, ALU.add, ALU.max))
                        v.tensor_copy(heads(carry)[:, :, 0:RUNS - 1], heads(inc)[:, :, 1:RUNS]).then_inc(s_row, 1)
                    dve.wait_ge(s_rowT, way + 1)
                    link(dve, v.tensor_copy(cols[:, 4 + way:5 + way], ps_c[:, 1, 0:1]))
                    link(dve, v.tensor_tensor_scan(mx_t if way == 0 else mx_t[:, ::-1], reset, data,
                                                   cols[:, 4 + way:5 + way], ALU.add, ALU.max))
                v.memset(E[:, RE:RE + P], 0.0).then_inc(s_max, 1)
                v.tensor_tensor(E[:, 0:cut], sc_t[:, 0:cut], mx_t[:, 0:cut], ALU.subtract).then_inc(s_dead, 1)
                dve.wait_ge(s_dead, 3)
                v.memset(R[:, 0:z1], 0.0).then_inc(s_zero, 1)

        s_voh = sem("v_onehot_ready")
        s_exp, s_exT, s_exc = sem("weights_ready"), sem("weights_transposed"), sem("weights_copied")
        s_pv, s_acc = sem("step_summed"), sem("step_added")
        loc_c = loc_t[:, 0:STEPS].rearrange("p (j c) -> p j c", c=RL)
        loc_n = loc_t[:, 1:STEPS + 1].rearrange("p (j c) -> p j c", c=RL)
        oht = oh[:, 1, :, :]
        exs = oh[:, 0, 4:6, :]
        exl = oh[:, 0, 6:8, :]

        with nc.psum_tensor("ps_a", [P, 2, 2, D], f32) as ps_a, \
                nc.psum_tensor("ps_ex", [P, 2, D], f32) as ps_ex, nc.Block(no_gpsimd_drain=True) as block:

            @block.sync
            def _(sp):
                def body(i):
                    for par in range(2):
                        c = 2 * i + par
                        wait(sp, s_wd, UN * (c + 1))
                        wait(sp, s_wa, UN * (c + 1))
                        load_vidx(sp, c + 2, par)

                repeat(sp, RL // 2 - 1, body)

            @block.gpsimd
            def _(pool):
                bound = pool.to_reg(BLOCKS * P - 1)

                def body(i):
                    for par in range(2):
                        for j in range(UN):
                            if not (isinstance(i, int) and par == 0 and j < RING):
                                gather(pool, i, par, j, bound)

                repeat(pool, RL // 2, body)

            @block.scalar
            def _(act):
                def weights(c, slot):
                    wait(act, s_exT, c - 1)
                    nc.scalar.activation(exs[:, slot, :], E[:, ds(c * P, P)], ACT.Exp, scale=DK ** -0.5).then_inc(s_exp, 1)

                def copies(c, slot):
                    wait(act, s_exT, c + 1)
                    wait(act, s_wa, UN * (c - 1))
                    nc.scalar.activation(exl[:, slot, :], ps_ex[:, slot, 0:P], ACT.Copy).then_inc(s_exc, 1)

                weights(0, 0)
                copies(0, 0)

                def body(i):
                    for par in range(2):
                        c = 2 * i + par
                        for j in range(UN):
                            s = UN * c + j
                            if j == 3:
                                weights(c + 1, 1 - par)
                            if j == 14:
                                copies(c + 1, 1 - par)
                            if j == 0:
                                wait(act, s_exc, c + 1)
                            wait(act, s_v[j % 8], 32 * c + 16 * (j // 8 + 1))
                            wait(act, s_pv, s - 3)
                            for h in range(MUL_HEADS, HEADS):
                                ins = nc.scalar.activation(prod[:, j % 4, h * DZ:(h + 1) * DZ],
                                                           ring[:, j % 8, h * DZ:(h + 1) * DZ], ACT.Copy,
                                                           scale=exl[:, par, h * RUNS + j:h * RUNS + j + 1])
                            ins.then_inc(s_wa, 1)

                repeat(act, RL // 2, body)

            @block.tensor
            def _(pe):
                def turn(c, slot):
                    wait(pe, s_exp, c + 1)
                    wait(pe, s_wd, UN * (c - 1))
                    wait(pe, s_exc, c - 1)
                    nc.tensor.transpose(ps_ex[:, slot, 0:P], exs[:, slot, :], ident[:]).then_inc(s_exT, 1)

                turn(0, 0)

                def body(i):
                    for par in range(2):
                        c = 2 * i + par
                        for j in range(UN):
                            s = UN * c + j
                            if j == 8:
                                turn(c + 1, 1 - par)
                            if j % 2 == 0:
                                wait(pe, s_voh, 8 * c + j // 2 + 1)
                            wait(pe, s_wd, s + 1)
                            wait(pe, s_wa, s + 1)
                            wait(pe, s_acc, s - 1)
                            for n in range(2):
                                ins = nc.tensor.matmul(ps_a[:, j % 2, n, 0:W // 2], oht[:, j % 8, :],
                                                       prod[:, j % 4, n * W // 2:(n + 1) * W // 2], start=True, stop=True)
                            ins.then_inc(s_pv, 1)

                repeat(pe, RL // 2, body)

            @block.vector
            def _(dve):
                v = nc.vector
                regs = [dve.alloc_register(f"dve_blk{u}") for u in range(8)]
                late = [dve.alloc_register(f"dve_late{u}") for u in range(4)]
                COLS = 4

                def add(s, n, blk):
                    to = q_blk[:, ds(blk, 1), :].rearrange("p a (n w) -> p (a n) w", n=2)
                    wait(dve, s_pv, s + 1)
                    wait(dve, s_acc, s)
                    v.tensor_tensor(to, to, ps_a[:, n % 2, :, 0:W // 2], ALU.add).then_inc(s_acc, 1)

                def onehot(loc2, slot):
                    v.tensor_tensor(oht[:, slot:slot + 2, :], iota_row[:].unsqueeze(1).to_broadcast([P, 2, P]),
                                    loc2.to_broadcast([P, 2, P]), ALU.is_equal).then_inc(s_voh, 1)

                def last_two():
                    return [dve.snap(r, min_val=0, max_val=BLOCKS - 1) for r in late[2:]]

                def body(i):
                    before = None if isinstance(i, int) else last_two()
                    for col in range(COLS):
                        c, par = COLS * i + col, col % 2
                        for j in range(UN):
                            s = UN * c + j
                            if j % 2 == 0:
                                wait(dve, s_pv, s - 2)
                                wait(dve, s_exc, c + 1)
                                for u in (j, j + 1):
                                    wait(dve, s_v[u % 8], 32 * c + 16 * (u // 8 + 1))
                                v.tensor_tensor(prod[:, j % 4:j % 4 + 2, 0:MUL_HEADS * DZ].rearrange("p s (h d) -> p s h d", h=MUL_HEADS),
                                                ring[:, j % 8:j % 8 + 2, 0:MUL_HEADS * DZ].rearrange("p s (h d) -> p s h d", h=MUL_HEADS),
                                                ps_ex[:, par, 0:P].rearrange("p (h j) -> p j h", h=HEADS)[:, j:j + 2, 0:MUL_HEADS]
                                                .unsqueeze(3).to_broadcast([P, 2, MUL_HEADS, DZ]), ALU.mult).then_inc(s_wd, 2)
                            n = UN * col + j - 2
                            if n >= 0:
                                if n % 8 == 0:
                                    blk = load8(dve, regs, blk_cols, COLS * UN * i + n)
                                add(s - 2, n, blk[n % 8])
                            elif before:
                                add(s - 2, n % 2, before[n + 2])
                            if j % 2 == 0:
                                onehot(loc_c[:, j + 2:j + 4, ds(c, 1)] if j < UN - 2 else loc_n[:, 0:2, ds(c, 1)], (j + 2) % 8)
                    dve.load(late, blk_cols[0:1, ds(COLS * UN * (i + 1) - 4, 4)])

                dve.wait_ge(s_zero, 4)
                onehot(loc_c[:, 0:2, 0:1], 0)
                repeat(dve, RL // COLS, body)
                for n, blk in enumerate(last_two()):
                    add(STEPS - 2 + n, n, blk)

        s_xa = [sem(f"x_for_residual1_in{i}") for i in range(2)]
        s_xb = [sem(f"x_for_residual2_in{i}") for i in range(2)]
        s_st = [sem(f"out_stored{i}") for i in range(2)]
        names = ("rz", "an", "aT", "aTc", "o", "t1", "mv1", "sd1", "rs1", "n1", "x1b", "xT", "xTc",
                 "h", "hr", "f", "t2", "mv2", "sd2", "rs2", "n2", "y", "mv3", "sd3", "fin")
        (f_rz, f_an, f_aT, f_aTc, f_o, f_t1, f_mv1, f_sd1, f_rs1, f_n1, f_x1b, f_xT, f_xTc,
         f_h, f_hr, f_f, f_t2, f_mv2, f_sd2, f_rs2, f_n2, f_y, f_mv3, f_sd3, f_fin) = (sem("finish_" + n) for n in names)
        f_z, f_g1, f_g2, f_o2, f_nm3 = (sem("finish_" + n) for n in ("z", "g1", "g2", "o2", "nm3"))
        f_bs = [sem(f"finish_bn_stats{n}") for n in range(3)]
        f_rc = [sem(f"finish_reciprocal{n}") for n in range(3)]

        def pairs(k):
            return [E[:, (2 * k + n) * D:(2 * k + n + 1) * D] for n in range(2)]

        an, aT, x1, x1T, x1b, t2 = (pairs(k) for k in range(6))
        xa, xb, outb = ([ring[:, 2 * k + n, 0:D] for n in range(2)] for k in range(3))
        hT = [oh[:, 0, 2 * n:2 * n + 2, :].rearrange("p a w -> p (a w)") for n in range(2)]
        g1, ob, g2, o2, _ = gains
        wo = wq
        zr = est[:, 0:2, 0:HEADS]
        stat = [[est[:, 2 + ln * 2 + n, :] for n in range(2)] for ln in range(3)]
        in_range = lambda t: not isinstance(t, int) or 0 <= t < BLOCKS

        with ExitStack() as banks, nc.Block(no_gpsimd_drain=True) as block:
            pb = lambda name: banks.enter_context(nc.psum_tensor(name, [P, D], f32))
            ps_aT, ps_o, ps_xT, ps_h0, ps_h1, ps_f = (pb(n) for n in ("ps_aT", "ps_o", "ps_xT", "ps_h0", "ps_h1", "ps_f"))
            ps_h = (ps_h0, ps_h1)

            def run(eng, period):
                for k in range(-1, 6):
                    period(k, k % 2)
                with eng.Fori(3, BLOCKS // 2) as i:
                    period(2 * i, 0)
                    period(2 * i + 1, 1)
                for k in range(BLOCKS - 1, BLOCKS + 3):
                    period(k, k % 2)

            @block.sync
            def _(sp):
                def period(k, slot):
                    t = k + 1
                    if in_range(t):
                        p = 1 - slot
                        wait(sp, f_t1, t - 1)
                        sp.dma_start(xa[p], a["x"][ds(t * P, P), :]).then_inc(s_xa[p], 16)
                    t = k - 1
                    if in_range(t):
                        p = 1 - slot
                        wait(sp, f_y, t - 1)
                        sp.dma_start(xb[p], a["x"][ds(t * P, P), :]).then_inc(s_xb[p], 16)
                    t = k - 4
                    if in_range(t) and not (isinstance(t, int) and t == BLOCKS - 1):
                        store(t, slot, P)

                def store(t, p, n):
                    wait(sp, f_fin, t + 1)
                    sp.dma_start(out[ds(t * P, n), :], outb[p][0:n, :]).then_inc(s_st[p], 16)

                run(sp, period)
                store(BLOCKS - 1, 0, NODES - (BLOCKS - 1) * P)
                sp.wait_ge(s_st[0], 16 * (BLOCKS // 2 + 1))
                sp.wait_ge(s_st[1], 16 * (BLOCKS // 2))

            @block.tensor
            def _(pe):
                def period(k, slot):
                    t, p = k - 1, 1 - slot
                    if in_range(t):
                        wait(pe, f_n1, t + 1)
                        wait(pe, f_xTc, t)
                        for c in range(KC):
                            ins = nc.tensor.transpose(ps_xT[:, c * P:(c + 1) * P], x1[p][:, c * P:(c + 1) * P], ident[:])
                        ins.then_inc(f_xT, 1)
                    t, p = k, slot
                    if in_range(t):
                        wait(pe, f_aTc, t + 1)
                        wait(pe, f_t1, t)
                        for c in range(KC):
                            ins = nc.tensor.matmul(ps_o[:], aT[p][:, c * P:(c + 1) * P], wo[:, c, :],
                                                   start=(c == 0), stop=(c == KC - 1))
                        ins.then_inc(f_o, 1)
                    t, p = k - 1, 1 - slot
                    if in_range(t):
                        wait(pe, f_xTc, t + 1)
                        for j in range(FC):
                            wait(pe, f_hr, 2 * t - 1 + j)
                            for c in range(KC):
                                ins = nc.tensor.matmul(ps_h[j][:, 0:P], w1[:, c, j * P:(j + 1) * P],
                                                       x1T[p][:, c * P:(c + 1) * P], start=(c == 0), stop=(c == KC - 1))
                            ins.then_inc(f_h, 1)
                    t, p = k + 1, 1 - slot
                    if in_range(t):
                        wait(pe, f_an, t + 1)
                        wait(pe, f_aTc, t)
                        for c in range(KC):
                            ins = nc.tensor.transpose(ps_aT[:, c * P:(c + 1) * P], an[p][:, c * P:(c + 1) * P], ident[:])
                        ins.then_inc(f_aT, 1)
                    t, p = k - 1, 1 - slot
                    if in_range(t):
                        wait(pe, f_t2, t)
                        for j in range(FC):
                            wait(pe, f_hr, 2 * t + j + 1)
                            ins = nc.tensor.matmul(ps_f[:], hT[p][:, j * P:(j + 1) * P], w2[:, j, :],
                                                   start=(j == 0), stop=(j == FC - 1))
                        ins.then_inc(f_f, 1)

                run(pe, period)

            @block.scalar
            def _(act):
                def root(s, src, done, n):
                    wait(act, src, n)
                    nc.scalar.activation(s[:, 8:9], s[:, 7:8], ACT.Sqrt, bias=eps[:]).then_inc(done, 1)

                def norm(s, x, src, done, n):
                    wait(act, src, n)
                    nc.scalar.activation(x, x, ACT.Identity, scale=s[:, 9:10], bias=s[:, 10:11]).then_inc(done, 1)

                def hidden(t, p, j):
                    wait(act, f_h, 2 * t + j + 1)
                    wait(act, f_f, t - 1)
                    nc.scalar.activation(hT[p][:, j * P:(j + 1) * P], ps_h[j][:, 0:P],
                                         ACT.Relu, bias=b1_col[:, j:j + 1]).then_inc(f_hr, 1)

                def period(k, slot):
                    t, p = k - 1, 1 - slot
                    if in_range(t):
                        wait(act, f_xT, t + 1)
                        wait(act, f_h, 2 * t - 2)
                        nc.scalar.activation(x1T[p], ps_xT[:], ACT.Copy).then_inc(f_xTc, 1)
                    t, p = k - 2, slot
                    if in_range(t):
                        root(stat[1][p], f_mv2, f_sd2, t + 1)
                        norm(stat[1][p], t2[p], f_rs2, f_n2, t + 1)
                    if in_range(k - 3):
                        root(stat[2][1 - slot], f_mv3, f_sd3, k - 2)
                    if in_range(k - 1):
                        hidden(k - 1, 1 - slot, 0)
                    if in_range(k):
                        root(stat[0][slot], f_mv1, f_sd1, k + 1)
                    if in_range(k - 1):
                        hidden(k - 1, 1 - slot, 1)
                    if in_range(k):
                        norm(stat[0][slot], x1[slot], f_rs1, f_n1, k + 1)
                    t, p = k + 1, 1 - slot
                    if in_range(t):
                        wait(act, f_aT, t + 1)
                        wait(act, f_o, t - 1)
                        nc.scalar.activation(aT[p], ps_aT[:], ACT.Copy).then_inc(f_aTc, 1)

                run(act, period)

            @block.gpsimd
            def _(pool):
                def period(k, slot):
                    t, p = k - 2, slot
                    if in_range(t):
                        wait(pool, f_g2, t + 1)
                        nc.gpsimd.tensor_tensor(t2[p], t2[p], o2, ALU.add).then_inc(f_o2, 1)
                        wait(pool, f_o2, t + 1)
                        wait(pool, s_xb[p], 8 * (t - p) + 16)
                        nc.gpsimd.tensor_tensor(t2[p], t2[p], xb[p], ALU.add).then_inc(f_y, 1)
                    t, p = k, slot
                    if in_range(t):
                        wait(pool, f_n1, t + 1)
                        wait(pool, f_t2, t - 1)
                        nc.gpsimd.tensor_tensor(x1b[p], x1[p], g1, ALU.mult).then_inc(f_g1, 1)
                        wait(pool, f_g1, t + 1)
                        nc.gpsimd.tensor_tensor(x1b[p], x1b[p], ob, ALU.add).then_inc(f_x1b, 1)

                run(pool, period)

            @block.vector
            def _(dve):
                v = nc.vector

                def stats(ln, p, x, ready, n):
                    wait(dve, ready, n)
                    v.bn_stats(stat[ln][p][:, 0:6], x).then_inc(f_bs[ln], 1)

                def mean_var(ln, p, n, done):
                    wait(dve, f_bs[ln], n)
                    dve.nop(nofuse=True)
                    v.bn_aggr(stat[ln][p][:, 6:8], stat[ln][p][:, 0:6]).then_inc(done, 1)

                def inverse(ln, p, ready, n):
                    wait(dve, ready, n)
                    v.reciprocal(stat[ln][p][:, 9:10], stat[ln][p][:, 8:9]).then_inc(f_rc[ln], 1)

                def shift(ln, p, n, done):
                    s = stat[ln][p]
                    wait(dve, f_rc[ln], n)
                    v.tensor_scalar(s[:, 10:11], s[:, 6:7], s[:, 9:10], -1.0, ALU.mult, ALU.mult).then_inc(done, 1)

                def period(k, slot):
                    new, now, mlp, end = (in_range(k + n) for n in (1, 0, -2, -3))
                    even, odd = slot, 1 - slot
                    heads = lambda: q_blk[:, ds(k + 1, 1), :].rearrange("p a (h d) -> p (a h) d", h=HEADS)
                    if mlp:
                        wait(dve, f_f, k - 1)
                        wait(dve, f_x1b, k - 1)
                        wait(dve, f_fin, k - 3)
                        v.tensor_tensor(t2[even], ps_f[:], x1b[even], ALU.add).then_inc(f_t2, 1)
                        stats(1, even, t2[even], f_t2, k - 1)
                    if new:
                        wait(dve, f_an, k)
                        wait(dve, f_rz, k)
                        v.tensor_scalar_max(zr[:, odd, :].unsqueeze(2), heads()[:, :, DK:DZ],
                                            1e-30).then_inc(f_z, 1)
                    if mlp:
                        mean_var(1, even, k - 1, f_mv2)
                    if end:
                        stats(2, odd, t2[odd], f_y, k - 2)
                    if new:
                        wait(dve, f_z, k + 2)
                        v.reciprocal(zr[:, odd, :], zr[:, odd, :]).then_inc(f_rz, 1)
                    if mlp:
                        inverse(1, even, f_sd2, k - 1)
                        shift(1, even, k - 1, f_rs2)
                    if new:
                        wait(dve, f_rz, k + 2)
                        wait(dve, f_aT, k)
                        v.tensor_tensor(an[odd].rearrange("p (h d) -> p h d", h=HEADS), heads()[:, :, 0:DK],
                                        zr[:, odd, :].unsqueeze(2).to_broadcast([P, HEADS, DK]), ALU.mult).then_inc(f_an, 1)
                    if end:
                        mean_var(2, odd, k - 2, f_mv3)
                    if now:
                        wait(dve, f_o, k + 1)
                        wait(dve, s_xa[even], 8 * (k - even) + 16)
                        wait(dve, f_g1, k - 1)
                        v.tensor_tensor(x1[even], ps_o[:], xa[even], ALU.add).then_inc(f_t1, 1)
                    if end:
                        inverse(2, odd, f_sd3, k - 2)
                    if now:
                        stats(0, even, x1[even], f_t1, k + 1)
                    if end:
                        shift(2, odd, k - 2, f_nm3)
                    if now:
                        mean_var(0, even, k + 1, f_mv1)
                    if mlp:
                        wait(dve, f_n2, k - 1)
                        v.tensor_tensor(t2[even], t2[even], g2, ALU.mult).then_inc(f_g2, 1)
                    if now:
                        inverse(0, even, f_sd1, k + 1)
                        shift(0, even, k + 1, f_rs1)
                    if end:
                        wait(dve, f_nm3, k - 2)
                        wait(dve, s_st[odd], 8 * (k - 3 - odd))
                        v.tensor_scalar(outb[odd], t2[odd], stat[2][odd][:, 9:10], stat[2][odd][:, 10:11],
                                        ALU.mult, ALU.add).then_inc(f_fin, 1)

                run(dve, period)


def kernel(**inputs):
    import numpy as np
    import concourse.bacc as bacc
    from concourse.bass_utils import run_bass_kernel_spmd

    g = {k.replace("L0_gnn_", ""): np.asarray(v) for k, v in inputs.items()}
    x = np.zeros((XT * P, D), g["x"].dtype)
    x[:NODES] = g["x"]
    n = TILES * P
    edges = np.zeros((3, n), g["src"].dtype)
    edges[0, :EDGES] = g["src"]
    edges[1, :] = BLOCKS * P - 1
    edges[1, :EDGES] = g["dst"]
    edges[2, 0] = -1
    edges[2, 1:] = edges[1, :-1]
    arrays = {
        "x": x,
        "xt": np.ascontiguousarray(x.reshape(XT, P, KC, P).transpose(0, 3, 2, 1)),
        "edges": np.ascontiguousarray(edges.reshape(3, TILES, P).transpose(1, 0, 2)).reshape(TILES, 3 * P),
        "tile_last": np.ascontiguousarray(edges[1].reshape(TILES, P)[:, -1]).reshape(1, TILES),
        "g1_col": np.ascontiguousarray(g["ln1_g"].reshape(KC, P).T),
        "o1_col": np.ascontiguousarray(g["ln1_b"].reshape(KC, P).T),
        "b1": np.ascontiguousarray(g["b1"].reshape(FC, P).T),
    }
    for name in ("Wq", "Wk", "Wv", "Wo", "W1", "W2"):
        w = g[name]
        arrays[name.lower()] = np.ascontiguousarray(w.reshape(w.shape[0] // P, P, w.shape[1]).transpose(1, 0, 2))
    for name in ("ln1_g", "ln1_b", "ln2_g", "ln2_b", "b2"):
        arrays[name] = g[name].reshape(1, D)
    nc = bacc.Bacc("TRN2", target_bir_lowering=False, num_devices=1)
    aps = {k: nc.dram_tensor("in_" + k, v.shape, mybir.dt.from_np(v.dtype), kind="ExternalInput").ap()
           for k, v in arrays.items()}
    out = nc.dram_tensor("out_0", (NODES, D), mybir.dt.float32, kind="ExternalOutput").ap()
    program(nc, aps, out)
    r = run_bass_kernel_spmd(nc, [{"in_" + k: v for k, v in arrays.items()}], core_ids=[0])
    return r.results[0]["out_0"]
```
